# Optimizing a Trainium2 kernel written in Bass

```python
import numpy as np
import jax
import jax.numpy as jnp

def _softmax(x, axis=-1):
    return jax.nn.softmax(x, axis=axis)

def _gelu(x):
    return jax.nn.gelu(x, approximate=True)

def _silu(x):
    return jax.nn.silu(x)

def _sigmoid(x):
    return jax.nn.sigmoid(x)

def _layernorm(x, axis=-1, eps=1e-05):
    m = jnp.mean(x, axis=axis, keepdims=True)
    v = jnp.var(x, axis=axis, keepdims=True)
    return (x - m) / jnp.sqrt(v + eps)

def _scatter_add(tgt, idx, src, axis=0):
    return tgt.at[idx].add(src)

def _segment_sum(src, seg, n):
    return jax.ops.segment_sum(src, seg, n)
kernel_name = 'mk_gnn_preln_d1_gnn_r8_bc4d4a'

def setup_inputs(seed: int=0):
    np.random.seed(seed)
    _w = jnp.asarray

    def _rec_inputs():
        import jax
        import jax.numpy as jnp
        _gk = jax.random.key(seed)
        x = -0.0009044 + 1 * jax.random.normal(jax.random.fold_in(_gk, 1), (12500, 32), jnp.float32)
        src = jax.random.randint(jax.random.fold_in(_gk, 2), (400000,), 0, 12500, jnp.int32)
        dst = jnp.minimum((12500 * jax.random.uniform(jax.random.fold_in(_gk, 3), (400000,)) ** 2.0).astype(jnp.int32), 99999)
        _o = jnp.argsort(dst, stable=True)
        src = src[_o]
        dst = dst[_o]
        edge_attr_2 = -5.09086e-05 + 0.577461 * jax.random.normal(jax.random.fold_in(_gk, 11), (400000, 2), jnp.float32)
        return (x, src, dst, edge_attr_2)
    x, src, dst, edge_attr_2 = _rec_inputs()

    def _L0_gnn_setup():
        import jax, jax.numpy as jnp
        import numpy as np
        N_NODES = 6250
        N_EDGES = 200000
        F_IN = 32
        F_OUT = 32
        BASIS = (4, 4)

        def _tent_basis(u, n):
            centers = jnp.linspace(-1.0, 1.0, n, dtype=u.dtype)
            h = 2.0 / (n - 1)
            return jnp.maximum(0.0, 1.0 - jnp.abs(u[:, None] - centers[None, :]) / h)
        key = jax.random.key(seed)
        k1, k2, k3, k4, k5 = jax.random.split(key, 5)
        x = jax.random.normal(k1, (N_NODES, F_IN), dtype=jnp.float32)
        edge_attr = jax.random.uniform(k2, (N_EDGES, 2), dtype=jnp.float32, minval=-1.0, maxval=1.0)
        weight = jax.random.uniform(k3, (*BASIS, F_IN, F_OUT), dtype=jnp.float32, minval=-0.05, maxval=0.05)
        src = jax.random.randint(k4, (N_EDGES,), 0, N_NODES)
        tgt = jax.random.randint(k5, (N_EDGES,), 0, N_NODES)
        edge_index = jnp.stack([tgt, src], axis=0).astype(jnp.int64)
        return {'x': x, 'edge_attr': edge_attr, 'weight': weight, 'edge_index': edge_index}
    _L0_gnn_all = _L0_gnn_setup()
    _L0_gnn_in = {k: v for k, v in _L0_gnn_all.items() if k in ('weight',)}
    del _L0_gnn_all
    return {'x': x, 'src': src, 'dst': dst, 'edge_attr_2': edge_attr_2, 'L0_gnn_weight': _L0_gnn_in['weight']}

def reference(x, src, dst, edge_attr_2, L0_gnn_weight):
    import jax
    import jax.numpy as jnp

    def _L0_gnn_ref(x, edge_attr, weight, edge_index):
        import jax, jax.numpy as jnp
        import numpy as np
        N_NODES = 6250
        N_EDGES = 200000
        F_IN = 32
        F_OUT = 32
        BASIS = (4, 4)

        def _tent_basis(u, n):
            centers = jnp.linspace(-1.0, 1.0, n, dtype=u.dtype)
            h = 2.0 / (n - 1)
            return jnp.maximum(0.0, 1.0 - jnp.abs(u[:, None] - centers[None, :]) / h)
        k1, k2, f_in, f_out = weight.shape
        n_nodes = x.shape[0]
        bu = _tent_basis(edge_attr[:, 0], k1)
        bv = _tent_basis(edge_attr[:, 1], k2)
        basis = (bu[:, :, None] * bv[:, None, :]).reshape(-1, k1 * k2)
        xj = x[edge_index[1]]
        w2 = weight.reshape(k1 * k2, f_in, f_out)
        msg = basis[:, 0:1] * (xj @ w2[0])
        for k in range(1, k1 * k2):
            msg = msg + basis[:, k:k + 1] * (xj @ w2[k])
        out = jax.ops.segment_sum(msg, edge_index[0], num_segments=n_nodes)
        return out
    edge_index = jnp.stack([src, dst])
    h = jnp.maximum(_layernorm(x, axis=-1), 0.0)
    x = x + _L0_gnn_ref(h, edge_attr_2, L0_gnn_weight, edge_index)
    return x

_drawn_inputs = setup_inputs


def setup_inputs(seed=0):
    import zlib

    import numpy as np

    out = dict(_drawn_inputs(seed))
    spreads = {}
    factors = {}
    for name, (base, spread) in spreads.items():
        noise = np.random.default_rng([zlib.crc32(name.encode()), seed]).standard_normal(out[name].shape)
        drawn = base * np.exp(spread * noise) if base else spread * noise
        out[name] = jnp.asarray(drawn.astype(out[name].dtype))
    for name, factor in factors.items():
        out[name] = (out[name] * factor).astype(out[name].dtype)
    return out
```

```python
from contextlib import ExitStack

import numpy as np

import concourse.bass as bass
from concourse import mybir

F32 = mybir.dt.float32
BF16 = mybir.dt.bfloat16
I32 = mybir.dt.int32
ALU = mybir.AluOpType
ACT = mybir.ActivationFunctionType
AX = mybir.AxisListType

P = 128
EPS = 1e-5


def edge_conv_kernel(nc, x, src, dst, attr, weight, out):
    N, F = x.shape
    E = src.shape[0]
    KU, KV, _, FO = weight.shape
    IO = KU * FO
    YROW = KV * IO
    WIN = P // KV
    SLOPE = (KU - 1) / 2.0
    TILES = E // P
    HT = (3, 2)
    H0 = (0, 3)
    RT = sum(HT)
    ROUNDS = TILES // RT
    HALVES = 2 * ROUNDS
    RE = RT * P
    NP = 125
    EP = E // NP
    RP = EP // RE
    TP = EP // P
    NN = N // NP
    NACC = RT
    AROWS = -(-(N + P) // (4 * P)) * 4 * P
    AR = AROWS // P
    assert E == ROUNDS * RE and EP == RP * RE and N == NP * NN and NN % 4 == 0
    NBLK = NN // 4
    NROW = 6
    LAST = HALVES - 1

    ctx = ExitStack()
    with ctx:
        def sb(name, shape, dt=F32):
            return ctx.enter_context(nc.sbuf_tensor(name, shape, dt))

        def sem(name):
            return ctx.enter_context(nc.semaphore(name))

        def dram(name, shape, dt=F32):
            return nc.dram_tensor(name, shape, dt, kind="Internal").ap()

        y_d = dram("y_table", (N, YROW))
        rows_d = dram("edge_rows", (NROW, E), BF16)
        base_d = dram("window_base", (ROUNDS, 4), I32)
        acc_d = [dram(f"accumulator_{b}", (AROWS, FO)) for b in range(NACC)]

        tent_u = sb("tent_u", [P, TILES, KU])
        src_col = sb("src_col", [P, TILES])
        ident = sb("ident", [P, P])
        tri = sb("tri", [P, P])
        node_col = sb("node_col", [P, 1])
        cv_col = sb("cv_col", [P, 1])
        cu = sb("cu", [P, KU])
        dummy_col = sb("dummy_col", [P, 1])
        int_col = sb("int_col", [P, 2], I32)
        sel = sb("sel", [NROW, 3, P], BF16)
        eps_col = sb("eps_col", [P, 1])
        ones_col = sb("ones_col", [P, 1])
        far_i = sb("far_i", [1, 1], I32)
        attr_n = sb("attr_n", [NP, EP, 2])
        src_m = sb("src_m", [P, EP], I32)
        dst_m = sb("dst_m", [P, EP], I32)
        src_n, dst_n = src_m[0:NP, :], dst_m[0:NP, :]
        src_f = sb("src_f", [NP, EP])
        r_n = sb("r_n", [NP, EP], BF16)
        parts_m = sb("parts_m", [P, 2 * (NROW - 1) * RE], BF16)
        parts = parts_m[0:NP, :].rearrange("p (s k e) -> p s k e", s=2, k=NROW - 1)
        rest = sb("rest", [NP, 2, RE])
        base_i = sb("base_i", [NP, RP, 4], I32)
        base_f = sb("base_f", [NP, RP, 2])
        span = sb("span", [NP, 4])
        zero = sb("zero", [P, AR * FO // 4])
        w_sb = sb("w_sb", [P, KV, KU, FO])
        stat = sb("stat", [NP, 3, NN])
        YST = 2
        ZN = 2 * NN * F + YST * 4 * YROW
        zone = sb("zone", [P, ZN])
        x_n = zone[0:NP, 0:NN * F]
        sq_n = zone[0:NP, NN * F:2 * NN * F]
        h_t = zone[:, NN * F:NN * F + NBLK * NP].rearrange("p (b n) -> p b n", n=NP)
        y_st = zone[:, 2 * NN * F:].rearrange("p (s g c) -> p s g c", s=YST, g=4)
        CMAX = HT[0] * P
        used = [0]

        def carve(cols):
            a = zone[:, used[0]:used[0] + cols]
            used[0] += cols
            assert used[0] <= ZN
            return a

        rows = [carve(CMAX // 2).bitcast(BF16)[0:NROW, :] for _ in range(4)]
        pick = [carve(CMAX) for _ in range(4)]
        same = [carve(CMAX) for _ in range(4)]
        prod = [carve(CMAX) for _ in range(2)]
        msg = [carve(HT[0] * FO) for _ in range(4)]
        summed = [carve(FO) for _ in range(2 * RT)]
        count = [carve(HT[0]) for _ in range(4)]
        moved = [carve(HT[0]) for _ in range(4)]
        row_idx = carve(2 * RT).bitcast(I32)
        shared = used[0]
        win = [carve(IO) for _ in range(4)]
        dist = [carve(CMAX) for _ in range(2)]
        tent_v = [carve(CMAX) for _ in range(4)]
        used[0] = shared
        yg = [carve(HT[0] * YROW) for _ in range(2)]
        tent_g = [carve(HT[0] * KV) for _ in range(2)]
        minus_g = [carve(HT[0] * KV) for _ in range(2)]
        dst_idx = carve(4 * HT[0]).bitcast(I32)
        v_col = parts_m[:, :].bitcast(F32)[:, 0:TILES]
        dst_f = src_m[0:NP, :].bitcast(F32)
        dst_col = dst_m[:, 0:TILES].bitcast(F32)
        bank = [ctx.enter_context(nc.psum_tensor(f"bank{i}", [P, 512], F32)) for i in range(8)]

        ps_v = [bank[0][:, 0:HT[0] * P], bank[1][:, 0:HT[1] * P]]
        ps_r = [bank[2][:, 0:HT[0] * P], bank[4][:, 256:256 + HT[1] * P]]
        ps_s = [bank[3][:, 0:HT[0] * P], bank[4][:, 0:HT[1] * P]]
        ps_g = [bank[5][:, 0:HT[0] * P], bank[6][:, 0:HT[1] * P]]
        ps_m = [bank[7][:, 0:HT[0] * FO], bank[7][:, 0:HT[1] * FO]]

        ld_x, ld_w, ld_src, ld_dst, ld_attr = (sem(f"ld_{n}") for n in ("x", "w", "src", "dst", "attr"))
        const_step, const_ready = sem("const_step"), sem("const_ready")
        ln_step, ln_done = sem("ln_step"), sem("ln_done")
        zero_ready = sem("zero_ready")
        src_cast = sem("src_cast")
        part_step, part_done = sem("part_step"), sem("part_done")
        part_out = [sem(f"part_out{i}") for i in range(2)]
        r_step, r_done, r_out = sem("r_step"), sem("r_done"), sem("r_out")
        base_done, base_out = sem("base_done"), sem("base_out")
        far_ps, far_ready = sem("far_ps"), sem("far_ready")
        col_ps, col_read = sem("col_ps"), sem("col_read")
        abs_u, tent_u_done = sem("abs_u"), sem("tent_u_done")
        ht_ps, ht_read = sem("ht_ps"), sem("ht_read")
        y_ps, y_copy_a, y_copy_v = sem("y_ps"), sem("y_copy_a"), sem("y_copy_v")
        y_out = [sem(f"y_out{i}") for i in range(YST)]
        s_rows = [sem(f"rows_in{i}") for i in range(4)]
        s_win = [sem(f"window_in{i}") for i in range(4)]
        s_gat = [sem(f"gathered{i}") for i in range(2)]
        v_ps, s_ps = sem("v_broadcast"), sem("r_src_broadcast")
        g_ps, m_ps = sem("gather_product"), sem("message_sums")
        dist_done, tv_done = sem("dist_done"), sem("tent_v_done")
        pick_done, same_done = sem("pick_done"), sem("same_done")
        prod_done, msg_done = sem("prod_done"), sem("msg_done")
        moved_done, idx_done = sem("moved_done"), sem("idx_done")
        sum_out = sem("sum_copied")
        landed = [sem(f"landed{b}") for b in range(NACC)]
        col2_ps, col2_free, col2_read, dst_cast = (sem(n) for n in ("col2_ps", "col2_free", "col2_read", "dst_cast"))
        tg_step, yg_mult, yg_done = sem("tg_step"), sem("yg_mult"), sem("yg_done")
        didx_done = sem("didx_done")
        scatter_turn, gather_turn = sem("scatter_turn"), sem("gather_turn")
        fin_in = [sem(f"fin_in{b}") for b in range(NACC)]
        fin_add, fin_out = sem("fin_add"), sem("fin_out")
        START = [32] + [16] * (NACC - 1)

        half_cols = [slice(H0[a] * P, (H0[a] + HT[a]) * P) for a in range(2)]

        def run_steps(eng, step, lead, lag):
            head = 6
            first = head // 2
            end = ROUNDS - 2 - (ROUNDS - 2 - first) % 2
            for h in range(-lead, head):
                step(h, h % 4, h // 2)
            with eng.Fori(first, end - 1, 2) as i:
                q = eng.snap(i)
                for k in range(4):
                    step(2 * q + k, (2 * first + k) % 4, q + k // 2)
            for h in range(2 * end, LAST + lag + 1):
                step(h, h % 4, h // 2)

        def inside(h, d):
            return not isinstance(h, int) or 0 <= h + d <= LAST

        def wait_half(eng, s, h, per=1):
            if not isinstance(h, int) or h >= 0:
                eng.wait_ge(s, h * per + per)

        def wait_slot(eng, s, h, slot, ring):
            if isinstance(h, int):
                eng.wait_ge(s, 16 * (h // ring + 1))
            else:
                eng.wait_ge(s, h * (16 // ring) + (16 - (slot % ring) * (16 // ring)))

        def tiles_of(q, a):
            return q * RT + H0[a]

        def cut(ap, start, n):
            return ap[:, start:start + n] if isinstance(start, int) else ap[:, bass.ds(start, n)]

        def fin_buf(b):
            if b < 3:
                part = NN * F // KU
                return tent_u[0:NP, b * part:(b + 1) * part, :].rearrange("p t i -> p (t i)")
            part = NN * F // 2
            return attr_n[:, (b - 3) * part:(b - 2) * part, :].rearrange("p e c -> p (e c)")

        block = ctx.enter_context(nc.Block())

        @block.sync
        def _(sp):
            sp.dma_start(x_n, x.rearrange("(p n) f -> p (n f)", p=NP)).then_inc(ld_x, 16)
            sp.dma_start(src_n[:, :], src.rearrange("(p e) -> p e", p=NP)).then_inc(ld_src, 16)
            sp.dma_start(attr_n[:, :, :], attr.rearrange("(p e) c -> p e c", p=NP)).then_inc(ld_attr, 16)
            for g in range(4):
                for i in range(KU):
                    sp.dma_start(w_sb[g * F:(g + 1) * F, :, i, :],
                                 weight[i].rearrange("j f o -> f j o")).then_inc(ld_w, 16)
            sp.dma_start(dst_n[:, :], dst.rearrange("(p e) -> p e", p=NP)).then_inc(ld_dst, 16)
            sp.wait_ge(base_done, 1)
            sp.dma_start(base_d.rearrange("(p r) c -> p r c", p=NP), base_i[:, :, :]).then_inc(base_out, 16)
            sp.wait_ge(r_done, 1)
            sp.dma_start(rows_d[0].rearrange("(p e) -> p e", p=NP), r_n[:, :]).then_inc(r_out, 16)
            rows_v = rows_d.rearrange("k (p c e) -> p k c e", p=NP, c=RP)
            y_v = y_d.rearrange("(p n) c -> p n c", p=NP)

            def store_parts(c):
                sp.wait_ge(part_done, c + 1)
                sp.dma_start(rows_v[:, 1:NROW, c, :], parts[:, c % 2, :, :]).then_inc(part_out[c % 2], 16)

            def store_y(b):
                sp.wait_ge(y_copy_a, 2 * (b + 1))
                sp.wait_ge(y_copy_v, 2 * (b + 1))
                sp.dma_start(y_v[:, 4 * b:4 * b + 4, :], y_st[0:NP, b % YST, :, :]).then_inc(y_out[b % YST], 16)

            for b in range(NBLK):
                if b % 3 == 0 and b // 3 < RP:
                    store_parts(b // 3)
                store_y(b)

            sp.wait_ge(base_out, 16)
            sp.wait_ge(r_out, 16)
            for i in range(2):
                sp.wait_ge(part_out[i], 16 * len(range(i, RP, 2)))
            for i in range(YST):
                sp.wait_ge(y_out[i], 16 * len(range(i, NBLK, YST)))
            sp.wait_ge(far_ready, 1)

            y_w = y_d.rearrange("n (j c) -> (n j) c", j=KV)

            def load_rows(h, slot, q, a):
                wait_half(sp, s_ps, h - 4)
                start = q * RE + H0[a] * P
                cols = HT[a] * P
                sp.dma_start(rows[slot][:, 0:cols], cut(rows_d, start, cols)).then_inc(s_rows[slot], 16)

            def window_step(base):
                def step(h, slot, q):
                    a = slot % 2
                    load_rows(h, slot, q, a)
                    if a == 0:
                        line = base_d[q:q + 1, 0:1] if isinstance(q, int) else base_d[bass.ds(q, 1), 0:1]
                        line2 = base_d[q:q + 1, 1:2] if isinstance(q, int) else base_d[bass.ds(q, 1), 1:2]
                        base[0] = sp.value_load(line, min_val=0, max_val=N - WIN)
                        base[1] = sp.value_load(line2, min_val=0, max_val=N - WIN)
                    wait_half(sp, g_ps, h - 4)
                    sp.dma_start(win[slot], y_w[bass.ds(base[a] * KV, P), :]).then_inc(s_win[slot], 16)
                return step

            far = sp.value_load(far_i[0:1, 0:1], min_val=0, max_val=1)
            with sp.If(far == 0):
                run_steps(sp, window_step([None, None]), 0, 0)
            with sp.Else():
                run_steps(sp, lambda h, slot, q: load_rows(h, slot, q, slot % 2), 0, 0)

            for b in range(NACC):
                sp.wait_ge(landed[b], START[b] + 16 * ROUNDS)
                dest = fin_buf(b)
                sp.dma_start(dest, acc_d[b][0:N, :].rearrange("(p n) f -> p (n f)", p=NP)).then_inc(fin_in[b], 16)
            sp.wait_ge(fin_add, NACC - 1)
            sp.dma_start(out.rearrange("(p n) f -> p (n f)", p=NP), fin_buf(0)).then_inc(fin_out, 16)
            sp.wait_ge(fin_out, 16)

        @block.gpsimd
        def _(pool):
            steps = [0]

            def chain(ins):
                ins.then_inc(const_step, 1)
                steps[0] += 1
                pool.wait_ge(const_step, steps[0])

            nc.gpsimd.memset(zero[:, :], 0.0).then_inc(zero_ready, 1)
            chain(nc.gpsimd.memset(ident[:, :], 0.0))
            chain(nc.gpsimd.affine_select(out=ident[:, :], in_=ident[:, :], compare_op=ALU.not_equal, fill=1.0,
                                          base=0, pattern=[[-1, P]], channel_multiplier=1))
            chain(nc.gpsimd.memset(tri[:, :], 1.0))
            chain(nc.gpsimd.affine_select(out=tri[:, :], in_=tri[:, :], compare_op=ALU.is_ge, fill=0.0,
                                          base=0, pattern=[[-1, P]], channel_multiplier=1))
            chain(nc.gpsimd.memset(sel[:, :, :], 1.0))
            for k, lo, hi in ((0, 0, 0), (1, 1, 3), (2, 4, NROW - 1)):
                chain(nc.gpsimd.affine_select(out=sel[:, k, :], in_=sel[:, k, :], compare_op=ALU.is_ge, fill=0.0,
                                              base=-lo, pattern=[[0, P]], channel_multiplier=1))
                chain(nc.gpsimd.affine_select(out=sel[:, k, :], in_=sel[:, k, :], compare_op=ALU.is_ge, fill=0.0,
                                              base=hi, pattern=[[0, P]], channel_multiplier=-1))
            chain(nc.gpsimd.iota(int_col[:, 0:1], pattern=[[0, 1]], base=0, channel_multiplier=1))
            nc.gpsimd.tensor_scalar(dummy_col[:, :], int_col[:, 0:1], float(N), None, ALU.add).then_inc(const_ready, 1)

            pool.dma_start(acc_d[0][0:N, :].rearrange("(p n) f -> p (n f)", p=NP),
                         x.rearrange("(p n) f -> p (n f)", p=NP)).then_inc(landed[0], 16)
            pool.wait_ge(zero_ready, 1)
            rest_rows = AROWS - N
            zp = max(d for d in range(1, P + 1) if rest_rows % d == 0)
            pool.dma_start(acc_d[0][N:AROWS, :].rearrange("(p n) f -> p (n f)", p=zp),
                         zero[0:zp, 0:rest_rows // zp * FO]).then_inc(landed[0], 16)
            zsrc = zero[:, :].unsqueeze(1).to_broadcast([P, 4, AR * FO // 4])
            for b in range(1, NACC):
                pool.dma_start(acc_d[b].rearrange("(p k n) f -> p k (n f)", p=P, k=4), zsrc)\
                  .then_inc(landed[b], 16)
            pool.wait_ge(ld_attr, 16)
            pool.wait_ge(src_cast, 1)
            n = [0]

            def link(ins):
                ins.then_inc(part_step, 1)
                n[0] += 1
                pool.wait_ge(part_step, n[0])

            for c in range(RP):
                s = c % 2
                if c >= 2:
                    pool.wait_ge(part_out[s], 16 * (c // 2))
                e = slice(c * RE, (c + 1) * RE)
                v = attr_n[:, e, 1]
                sf = src_f[:, e]
                link(nc.gpsimd.tensor_copy(parts[:, s, 0, :], v))
                link(nc.gpsimd.tensor_tensor(rest[:, 0, :], v, parts[:, s, 0, :], ALU.subtract))
                link(nc.gpsimd.tensor_copy(parts[:, s, 1, :], rest[:, 0, :]))
                link(nc.gpsimd.tensor_copy(parts[:, s, 3, :], sf))
                link(nc.gpsimd.tensor_tensor(parts[:, s, 2, :], rest[:, 0, :], parts[:, s, 1, :], ALU.subtract))
                nc.gpsimd.tensor_tensor(parts[:, s, 4, :], sf, parts[:, s, 3, :], ALU.subtract).then_inc(part_done, 1)

            for i in range(YST):
                pool.wait_ge(y_out[i], 16 * len(range(i, NBLK, YST)))
            pool.wait_ge(far_ready, 1)

            def scatter(h, slot, q):
                a = slot % 2
                wait_half(pool, sum_out, h)
                wait_half(pool, idx_done, h)
                for b in range(H0[a], H0[a] + HT[a]):
                    pool.wait_ge(landed[b], q * 16 + START[b])
                pool.sem_inc(scatter_turn, 1)
                for t in range(HT[a]):
                    b = H0[a] + t
                    k = (slot // 2) * RT + b
                    idx = row_idx[:, k:k + 1]
                    pool.indirect_dma_start(acc_d[b], bass.IndirectOffsetOnAxis(ap=idx, axis=0),
                                            summed[k], None,
                                            compute_op=ALU.add).then_inc(landed[b], 16)

            def gather_scatter(h, slot, q):
                if inside(h, 2):
                    a = slot % 2
                    slot2 = (slot + 2) % 4
                    wait_half(pool, yg_done, h)
                    wait_half(pool, didx_done, h + 2)
                    pool.sem_inc(gather_turn, 1)
                    for t in range(HT[a]):
                        k = slot2 * HT[0] + t
                        idx = dst_idx[:, k:k + 1]
                        pool.indirect_dma_start(yg[a][:, t * YROW:(t + 1) * YROW], None, y_d,
                                                bass.IndirectOffsetOnAxis(ap=idx, axis=0)).then_inc(s_gat[a], 16)
                if inside(h, 0):
                    scatter(h, slot, q)

            far = pool.value_load(far_i[0:1, 0:1], min_val=0, max_val=1)
            with pool.If(far == 0):
                run_steps(pool, scatter, 0, 0)
            with pool.Else():
                run_steps(pool, gather_scatter, 2, 0)

        NCB = -(-TP // 4)

        def columns(c):
            m = min(4, TP - 4 * c)
            return m

        @block.scalar
        def _(act):
            act.wait_ge(ld_src, 16)
            nc.scalar.copy(src_f[:, :], src_n[:, :]).then_inc(src_cast, 1)
            act.wait_ge(const_ready, 2)
            for c in range(NCB):
                m = columns(c)
                act.wait_ge(col_ps, 2 * c + 1)
                dest = src_col[:, :].rearrange("p (a k) -> p k a", k=TP)[:, 4 * c:4 * c + m, :]
                nc.scalar.copy(dest, bank[6][:, 0:m * NP].rearrange("p (k a) -> p k a", k=m)).then_inc(col_read, 1)
                act.wait_ge(col_ps, 2 * c + 2)
                for i in range(KU):
                    dest = tent_u[:, :, i].rearrange("p (a k) -> p k a", k=TP)[:, 4 * c:4 * c + m, :]
                    last = nc.scalar.activation(dest, bank[7][:, 0:m * NP].rearrange("p (k a) -> p k a", k=m),
                                                ACT.Abs, bias=cu[:, i:i + 1], scale=1.0)
                last.then_inc(col_read, 1)
            act.wait_ge(col_read, 2 * NCB)
            flat = tent_u[:, :, :].rearrange("p t i -> p (t i)")
            nc.scalar.activation(flat, flat, ACT.Relu, bias=ones_col[:, :], scale=-SLOPE).then_inc(tent_u_done, 1)
            act.wait_ge(ln_step, 3)
            nc.scalar.activation(sq_n, x_n, ACT.Square).then_inc(ln_step, 1)
            act.wait_ge(ln_step, 5)
            nc.scalar.activation(stat[:, 1, :], stat[:, 2, :], ACT.Sqrt, bias=eps_col[0:NP, :], scale=1.0 / F)\
              .then_inc(ln_step, 1)
            for b in range(NBLK):
                if b >= YST:
                    act.wait_ge(y_out[b % YST], 16 * (b // YST))
                for g in (1, 3):
                    act.wait_ge(y_ps, 4 * b + g + 1)
                    nc.scalar.copy(y_st[0:NP, b % YST, g, :], bank[2 + g][0:NP, :]).then_inc(y_copy_a, 1)
            for i in range(YST):
                act.wait_ge(y_out[i], 16 * len(range(i, NBLK, YST)))
            act.wait_ge(far_ready, 1)

            def tents(h, slot):
                a = slot % 2
                cols = HT[a] * P
                wait_half(act, v_ps, h)
                wait_half(act, tv_done, h - 2)
                nc.scalar.activation(dist[a][:, 0:cols], ps_v[a], ACT.Abs, bias=cv_col[:, :], scale=1.0)\
                  .then_inc(dist_done, 1)
                wait_half(act, pick_done, h - 4)
                wait_half(act, dist_done, h)
                nc.scalar.activation(tent_v[slot][:, 0:cols], dist[a][:, 0:cols], ACT.Relu,
                                     bias=ones_col[:, :], scale=-SLOPE).then_inc(tv_done, 1)

            def copy_sums(h, slot, q):
                a = slot % 2
                wait_half(act, m_ps, h)
                if not isinstance(h, int) or h >= 4:
                    for b in range(H0[a], H0[a] + HT[a]):
                        act.wait_ge(landed[b], q * 16 + START[b] - 16)
                for t in range(HT[a]):
                    ins = nc.scalar.copy(summed[(slot // 2) * RT + H0[a] + t], ps_m[a][:, t * FO:(t + 1) * FO])
                ins.then_inc(sum_out, 1)

            def step(h, slot, q, windows=True):
                if windows and inside(h, 1):
                    tents(h + 1, (slot + 1) % 4)
                if inside(h, -2):
                    copy_sums(h - 2, (slot - 2) % 4, q - 1)

            far = act.value_load(far_i[0:1, 0:1], min_val=0, max_val=1)
            with act.If(far == 0):
                run_steps(act, step, 1, 2)
            with act.Else():
                run_steps(act, lambda h, slot, q: step(h, slot, q, False), 0, 2)

        @block.vector
        def _(dve):
            nc.vector.memset(ones_col[:, :], 1.0)
            nc.vector.memset(eps_col[:, :], EPS)
            for i in range(KU):
                last = nc.vector.memset(cu[:, i:i + 1], 1.0 - 2.0 * i / (KU - 1))
            last.then_inc(const_ready, 1)
            dve.wait_ge(ld_x, 16)
            x3 = x_n.rearrange("p (n f) -> p n f", f=F)
            sq3 = sq_n.rearrange("p (n f) -> p n f", f=F)
            wide = [NP, NN, F]
            nc.vector.tensor_reduce(stat[:, 0, :], x3, AX.X, ALU.add).then_inc(ln_step, 1)
            dve.wait_ge(ln_step, 1)
            nc.vector.tensor_scalar(stat[:, 1, :], stat[:, 0, :], 1.0 / F, None, ALU.mult).then_inc(ln_step, 1)
            dve.wait_ge(ln_step, 2)
            nc.vector.tensor_tensor(x3, x3, stat[:, 1, :].unsqueeze(2).to_broadcast(wide), ALU.subtract)\
              .then_inc(ln_step, 1)
            dve.wait_ge(ln_step, 4)
            nc.vector.tensor_reduce(stat[:, 2, :], sq3, AX.X, ALU.add).then_inc(ln_step, 1)
            dve.wait_ge(ln_step, 6)
            nc.vector.reciprocal(stat[:, 0, :], stat[:, 1, :]).then_inc(ln_step, 1)
            dve.wait_ge(ln_step, 7)
            nc.vector.scalar_tensor_tensor(out=x3, in0=x3, scalar=0.0,
                                           in1=stat[:, 0, :].unsqueeze(2).to_broadcast(wide),
                                           op0=ALU.max, op1=ALU.mult).then_inc(ln_done, 1)
            dve.wait_ge(const_ready, 2)
            nc.vector.tensor_scalar(int_col[:, 1:2], int_col[:, 0:1], 2, None, ALU.arith_shift_right)\
              .then_inc(r_step, 1)
            dve.wait_ge(r_step, 1)
            nc.vector.tensor_copy(node_col[:, :], int_col[:, 1:2]).then_inc(r_step, 1)
            dve.wait_ge(r_step, 2)
            nc.vector.tensor_scalar(int_col[:, 1:2], int_col[:, 0:1], KV - 1, None, ALU.bitwise_and)\
              .then_inc(r_step, 1)
            dve.wait_ge(r_step, 3)
            nc.vector.tensor_scalar(cv_col[:, :], int_col[:, 1:2], -2.0 / (KV - 1), 1.0, ALU.mult, ALU.add)\
              .then_inc(r_step, 1)
            dve.wait_ge(ld_dst, 16)
            d5 = dst_n[:, :].rearrange("p (r t e) -> p r t e", r=RP, t=RT)
            nc.vector.memset(base_i[:, :, :], 0).then_inc(r_step, 1)
            dve.wait_ge(r_step, 5)
            for a in range(2):
                nc.vector.tensor_scalar(base_f[:, :, a], d5[:, :, H0[a], 0], float(N - WIN), None, ALU.min)
                last = nc.vector.tensor_scalar(base_i[:, :, a], d5[:, :, H0[a], 0], float(N - WIN), None, ALU.min)
            last.then_inc(base_done, 1)
            dve.wait_ge(base_done, 1)
            dr = dst_n[:, :].rearrange("p (r c) -> p r c", r=RP)
            rr = r_n[:, :].rearrange("p (r c) -> p r c", r=RP)
            for a in range(2):
                last = nc.vector.tensor_tensor(rr[:, :, half_cols[a]], dr[:, :, half_cols[a]],
                                               base_f[:, :, a:a + 1].to_broadcast([NP, RP, HT[a] * P]), ALU.subtract)
            last.then_inc(r_done, 1)
            dve.wait_ge(r_done, 1)
            nc.vector.tensor_reduce(span[:, 0:1], r_n[:, :], AX.X, ALU.min)
            nc.vector.tensor_reduce(span[:, 1:2], r_n[:, :], AX.X, ALU.max).then_inc(r_step, 1)
            dve.wait_ge(r_step, 6)
            nc.vector.tensor_scalar(span[:, 0:1], span[:, 0:1], 0.0, None, ALU.is_lt)
            nc.vector.tensor_scalar(span[:, 1:2], span[:, 1:2], float(WIN - 1), None, ALU.is_gt).then_inc(r_step, 1)
            dve.wait_ge(r_step, 7)
            nc.vector.tensor_tensor(span[:, 2:3], span[:, 0:1], span[:, 1:2], ALU.add).then_inc(r_step, 1)
            for b in range(NBLK + 1):
                if b < NBLK:
                    dve.wait_ge(ht_ps, b + 1)
                    nc.vector.tensor_copy(h_t[:, b, :], bank[b % 2][:, 0:NP]).then_inc(ht_read, 1)
                if b >= 1:
                    c = b - 1
                    if c >= YST:
                        dve.wait_ge(y_out[c % YST], 16 * (c // YST))
                    for g in (0, 2):
                        dve.wait_ge(y_ps, 4 * c + g + 1)
                        nc.vector.tensor_copy(y_st[0:NP, c % YST, g, :], bank[2 + g][0:NP, :]).then_inc(y_copy_v, 1)
            dve.wait_ge(far_ps, 1)
            nc.vector.tensor_scalar(far_i[0:1, 0:1], bank[0][0:1, 0:1], 1.0, None, ALU.min).then_inc(far_ready, 1)
            dve.wait_ge(far_ready, 1)
            for i in range(YST):
                dve.wait_ge(y_out[i], 16 * len(range(i, NBLK, YST)))
            dve.wait_ge(tent_u_done, 1)
            dve.wait_ge(part_done, RP)

            def build_pick(h, slot):
                a = slot % 2
                cols = HT[a] * P
                wait_half(dve, s_ps, h)
                wait_half(dve, tv_done, h)
                wait_half(dve, g_ps, h - 4)
                nc.vector.scalar_tensor_tensor(out=pick[slot][:, 0:cols], in0=ps_r[a], scalar=node_col[:, :],
                                               in1=tent_v[slot][:, 0:cols], op0=ALU.is_equal, op1=ALU.mult)\
                  .then_inc(pick_done, 1)

            def build_same(h, slot, q):
                a = slot % 2
                wait_half(dve, s_ps, h)
                wait_half(dve, m_ps, h - 4)
                wait_half(dve, moved_done, h - 4)
                for t in range(HT[a]):
                    ins = nc.vector.scalar_tensor_tensor(
                        out=same[slot][:, t * P:(t + 1) * P], in0=ps_s[a][:, t * P:(t + 1) * P],
                        scalar=cut(src_col, tiles_of(q, a) + t, 1), in1=tri[:, :],
                        op0=ALU.is_equal, op1=ALU.mult, accum_out=count[slot][:, t:t + 1])
                ins.then_inc(same_done, 1)

            def weigh(h, slot, q):
                a = slot % 2
                n = HT[a]
                if far_form[0]:
                    g_in = pick[slot][:, 0:n * P]
                    wait_half(dve, yg_done, h)
                else:
                    g_in = ps_g[a]
                    wait_half(dve, g_ps, h)
                wait_half(dve, msg_done, h - 2)
                tu = cut(tent_u, tiles_of(q, a), n).rearrange("p t i -> p (t i)")
                nc.vector.tensor_tensor(prod[a][:, 0:n * IO].rearrange("p (k o) -> p k o", o=FO),
                                        g_in.rearrange("p (k o) -> p k o", o=FO),
                                        tu.unsqueeze(2).to_broadcast([P, n * KU, FO]), ALU.mult).then_inc(prod_done, 1)

            def sum_i(h, slot):
                a = slot % 2
                n = HT[a]
                wait_half(dve, prod_done, h)
                wait_half(dve, m_ps, h - 4)
                nc.vector.tensor_reduce(msg[slot][:, 0:n * FO].rearrange("p (t o) -> p t o", o=FO),
                                        prod[a][:, 0:n * IO].rearrange("p (t i o) -> p t o i", t=n, i=KU),
                                        AX.X, ALU.add).then_inc(msg_done, 1)

            def mark_repeats(h, slot):
                a = slot % 2
                n = HT[a]
                wait_half(dve, same_done, h)
                wait_half(dve, idx_done, h - 4)
                nc.vector.scalar_tensor_tensor(out=moved[slot][:, 0:n], in0=count[slot][:, 0:n], scalar=1.0,
                                               in1=dummy_col[:, :].to_broadcast([P, n]),
                                               op0=ALU.is_gt, op1=ALU.mult).then_inc(moved_done, 1)

            def choose_rows(h, slot, q):
                a = slot % 2
                n = HT[a]
                wait_half(dve, moved_done, h)
                t0 = tiles_of(q, a)
                if not isinstance(h, int) or h >= 4:
                    for b in range(H0[a], H0[a] + n):
                        dve.wait_ge(landed[b], q * 16 + START[b] - 16)
                k = (slot // 2) * RT + H0[a]
                nc.vector.tensor_tensor(row_idx[:, k:k + n], moved[slot][:, 0:n], cut(src_col, t0, n), ALU.max)\
                  .then_inc(idx_done, 1)

            far_form = [False]

            def combine(h, slot, q):
                a = slot % 2
                n = HT[a]
                tg = tent_g[a][:, 0:n * KV].rearrange("p (t j) -> p t j", j=KV)
                wait_half(dve, yg_done, h - 2)
                nc.vector.tensor_tensor(tg, cut(v_col, tiles_of(q, a), n).unsqueeze(2).to_broadcast([P, n, KV]),
                                        cu[:, :].unsqueeze(1).to_broadcast([P, n, KV]), ALU.add).then_inc(tg_step, 1)
                dve.wait_ge(tg_step, h * 4 + 1)
                flat = tent_g[a][:, 0:n * KV]
                nc.vector.tensor_scalar(minus_g[a][:, 0:n * KV], flat, -1.0, None, ALU.mult).then_inc(tg_step, 1)
                dve.wait_ge(tg_step, h * 4 + 2)
                nc.vector.tensor_tensor(flat, flat, minus_g[a][:, 0:n * KV], ALU.max).then_inc(tg_step, 1)
                dve.wait_ge(tg_step, h * 4 + 3)
                nc.vector.tensor_scalar(flat, flat, -SLOPE, 1.0, ALU.mult, ALU.add).then_inc(tg_step, 1)
                dve.wait_ge(tg_step, h * 4 + 4)
                dve.wait_ge(s_gat[a], q * (16 * n) + 16 * n)
                y4 = yg[a][:, 0:n * YROW].rearrange("p (k c) -> p k c", c=IO)
                nc.vector.scalar_tensor_tensor(out=y4, in0=flat.unsqueeze(2).to_broadcast([P, n * KV, IO]), scalar=0.0,
                                               in1=y4, op0=ALU.max, op1=ALU.mult).then_inc(yg_mult, 1)
                wait_half(dve, yg_mult, h)
                for t in range(n):
                    ins = nc.vector.tensor_reduce(pick[slot][:, t * P:(t + 1) * P],
                                                  yg[a][:, t * YROW:(t + 1) * YROW].rearrange("p (j c) -> p c j", j=KV),
                                                  AX.X, ALU.add)
                ins.then_inc(yg_done, 1)

            def index_dst(h, slot, q):
                a = slot % 2
                wait_half(dve, yg_mult, h - 4)
                nc.vector.tensor_copy(dst_idx[:, slot * HT[0]:slot * HT[0] + HT[a]],
                                      cut(dst_col, tiles_of(q, a), HT[a])).then_inc(didx_done, 1)

            def step(h, slot, q):
                if far_form[0] and inside(h, 4):
                    index_dst(h + 4, slot, q + 2)
                if inside(h, 0):
                    if far_form[0]:
                        combine(h, slot, q)
                    else:
                        build_pick(h, slot)
                    build_same(h, slot, q)
                if inside(h, -1):
                    weigh(h - 1, (slot - 1) % 4, q - (1 - slot % 2))
                if inside(h, 0):
                    mark_repeats(h, slot)
                if inside(h, -1):
                    sum_i(h - 1, (slot - 1) % 4)
                if inside(h, 0):
                    choose_rows(h, slot, q)

            far = dve.value_load(far_i[0:1, 0:1], min_val=0, max_val=1)
            with dve.If(far == 0):
                run_steps(dve, step, 0, 1)
            with dve.Else():
                far_form[0] = True
                nc.vector.tensor_copy(dst_f, dst_n[:, :]).then_inc(dst_cast, 1)
                for c in range(NCB):
                    m = columns(c)
                    dve.wait_ge(col2_ps, c + 1)
                    for k, dest in enumerate((dst_col, v_col)):
                        last = nc.vector.tensor_copy(
                            dest.rearrange("p (a k) -> p k a", k=TP)[:, 4 * c:4 * c + m, :],
                            bank[6 + k][:, 0:m * NP].rearrange("p (k a) -> p k a", k=m))
                    if c < NCB - 1:
                        last.then_inc(col2_free, 1)
                    else:
                        last.then_inc(col2_read, 1)
                dve.wait_ge(col2_read, 1)
                run_steps(dve, step, 4, 1)

            dve.wait_ge(fin_in[0], 16)
            for b in range(1, NACC):
                dve.wait_ge(fin_in[b], 16)
                if b >= 2:
                    dve.wait_ge(fin_add, b - 1)
                nc.vector.tensor_tensor(fin_buf(0), fin_buf(0), fin_buf(b), ALU.add).then_inc(fin_add, 1)

        @block.tensor
        def _(pe):
            idn = ident[0:NP, 0:NP]
            pe.wait_ge(const_ready, 2)
            pe.wait_ge(src_cast, 1)
            pe.wait_ge(ld_attr, 16)
            for c in range(NCB):
                m = columns(c)
                for k in range(2):
                    if c >= 1:
                        pe.wait_ge(col_read, 2 * c - 1 + k)
                    for t in range(m):
                        e = slice((4 * c + t) * P, (4 * c + t + 1) * P)
                        ins = nc.tensor.transpose(bank[6 + k][:, t * NP:(t + 1) * NP],
                                                  src_f[:, e] if k == 0 else attr_n[:, e, 0], idn)
                    ins.then_inc(col_ps, 1)
            pe.wait_ge(ln_done, 1)
            pe.wait_ge(ld_w, 16 * 4 * KU)

            def turn(b):
                if b >= 2:
                    pe.wait_ge(ht_read, b - 1)
                nc.tensor.transpose(bank[b % 2][:, 0:NP], x_n[:, b * P:(b + 1) * P], idn).then_inc(ht_ps, 1)

            turn(0)
            for b in range(NBLK):
                if b + 1 < NBLK:
                    turn(b + 1)
                pe.wait_ge(ht_read, b + 1)
                for g in range(4):
                    if b >= 1:
                        pe.wait_ge((y_copy_v, y_copy_a)[g % 2], 2 * (b - 1) + g // 2 + 1)
                    nc.tensor.matmul(bank[2 + g][0:NP, :], h_t[g * F:(g + 1) * F, b, :],
                                     w_sb[g * F:(g + 1) * F, :, :, :].rearrange("p j i o -> p (j i o)"),
                                     start=True, stop=True, tile_position=(g * F, 0)).then_inc(y_ps, 1)
            pe.wait_ge(r_step, 8)
            pe.wait_ge(ht_read, NBLK)
            nc.tensor.matmul(bank[0][0:1, 0:1], span[:, 2:3], ones_col[0:NP, :], start=True, stop=True)\
              .then_inc(far_ps, 1)
            pe.wait_ge(far_ready, 1)
            pe.wait_ge(y_copy_a, 2 * NBLK)
            pe.wait_ge(y_copy_v, 2 * NBLK)
            pe.wait_ge(col_read, 2 * NCB)

            def broadcast(h, slot, windows):
                a = slot % 2
                cols = HT[a] * P
                wait_slot(pe, s_rows[slot], h, slot, 4)
                rhs = rows[slot][:, 0:cols]
                if windows:
                    wait_half(pe, dist_done, h - 2)
                    nc.tensor.matmul(ps_v[a], sel[:, 1, :], rhs, start=True, stop=True).then_inc(v_ps, 1)
                wait_half(pe, same_done, h - 2)
                if windows:
                    nc.tensor.matmul(ps_r[a], sel[:, 0, :], rhs, start=True, stop=True)
                nc.tensor.matmul(ps_s[a], sel[:, 2, :], rhs, start=True, stop=True).then_inc(s_ps, 1)

            def gather(h, slot):
                a = slot % 2
                wait_half(pe, pick_done, h)
                wait_slot(pe, s_win[slot], h, slot, 4)
                wait_half(pe, prod_done, h - 2)
                for t in range(HT[a]):
                    ins = nc.tensor.matmul(ps_g[a][:, t * P:(t + 1) * P], pick[slot][:, t * P:(t + 1) * P],
                                           win[slot], start=True, stop=True)
                ins.then_inc(g_ps, 1)

            def sum_same(h, slot):
                a = slot % 2
                wait_half(pe, same_done, h)
                wait_half(pe, msg_done, h)
                wait_half(pe, sum_out, h - 1)
                for t in range(HT[a]):
                    ins = nc.tensor.matmul(ps_m[a][:, t * FO:(t + 1) * FO], same[slot][:, t * P:(t + 1) * P],
                                           msg[slot][:, t * FO:(t + 1) * FO], start=True, stop=True)
                ins.then_inc(m_ps, 1)

            def step(h, slot, q, windows=True):
                if inside(h, 1):
                    broadcast(h + 1, (slot + 1) % 4, windows)
                if windows and inside(h, 0):
                    gather(h, slot)
                if inside(h, -1):
                    sum_same(h - 1, (slot - 1) % 4)

            far = pe.value_load(far_i[0:1, 0:1], min_val=0, max_val=1)
            with pe.If(far == 0):
                run_steps(pe, step, 1, 1)
            with pe.Else():
                pe.wait_ge(dst_cast, 1)
                for c in range(NCB):
                    m = columns(c)
                    if c >= 1:
                        pe.wait_ge(col2_free, c)
                    for k in range(2):
                        for t in range(m):
                            e = slice((4 * c + t) * P, (4 * c + t + 1) * P)
                            ins = nc.tensor.transpose(bank[6 + k][:, t * NP:(t + 1) * NP],
                                                      dst_f[:, e] if k == 0 else attr_n[:, e, 1], idn)
                    ins.then_inc(col2_ps, 1)
                pe.wait_ge(col2_read, 1)
                run_steps(pe, lambda h, slot, q: step(h, slot, q, False), 1, 1)


_INS = ["x", "src", "dst", "edge_attr_2", "L0_gnn_weight"]


def kernel(**inputs):
    import concourse.bacc as _bacc
    from concourse.bass_utils import run_bass_kernel_spmd as _run

    nc = _bacc.Bacc("TRN2", target_bir_lowering=False, num_devices=1)
    arrays, args = {}, []
    for name in _INS:
        a = np.ascontiguousarray(inputs[name])
        arrays[f"in_{name}"] = a
        args.append(nc.dram_tensor(f"in_{name}", a.shape, mybir.dt.from_np(a.dtype), kind="ExternalInput").ap())
    shape = inputs["x"].shape
    args.append(nc.dram_tensor("out_x", shape, F32, kind="ExternalOutput").ap())
    edge_conv_kernel(nc, *args)
    r = _run(nc, [arrays], core_ids=[0])
    return r.results[0]["out_x"]
```

```python
from contextlib import ExitStack

import numpy as np

import concourse.bass as bass
from concourse import mybir

F32 = mybir.dt.float32
BF16 = mybir.dt.bfloat16
I32 = mybir.dt.int32
U8 = mybir.dt.uint8
U16 = mybir.dt.uint16
ALU = mybir.AluOpType
ACT = mybir.ActivationFunctionType
AX = mybir.AxisListType

P = 128
EPS = 1e-5


def edge_conv_kernel(nc, x, src, dst, attr, weight, out):
    N, F = x.shape
    E = src.shape[0]
    KU, KV, _, FO = weight.shape
    IO = KU * FO
    YROW = KV * IO
    WIN = P // KV
    SLOPE = (KU - 1) / 2.0
    TILES = E // P
    HT = (3, 2)
    H0 = (0, 3)
    RT = sum(HT)
    ROUNDS = TILES // RT
    HALVES = 2 * ROUNDS
    RE = RT * P
    NP = 125
    EP = E // NP
    RP = EP // RE
    TP = EP // P
    NN = N // NP
    NACC = RT
    AROWS = -(-(N + P) // (4 * P)) * 4 * P
    AR = AROWS // P
    assert E == ROUNDS * RE and EP == RP * RE and N == NP * NN and NN % 4 == 0
    NBLK = NN // 4
    NPART = 3
    LAST = HALVES - 1

    ctx = ExitStack()
    with ctx:
        def sb(name, shape, dt=F32):
            return ctx.enter_context(nc.sbuf_tensor(name, shape, dt))

        def sem(name):
            return ctx.enter_context(nc.semaphore(name))

        def dram(name, shape, dt=F32):
            return nc.dram_tensor(name, shape, dt, kind="Internal").ap()

        y_d = dram("y_table", (N, YROW))
        vrow_d = dram("v_parts", (NPART, E), BF16)
        rs_d = dram("r_and_src", (ROUNDS, 3 * RE), U8)
        base_d = dram("window_base", (ROUNDS, 4), I32)
        acc_d = [dram(f"accumulator_{b}", (AROWS, FO)) for b in range(NACC)]

        tent_u = sb("tent_u", [P, TILES, KU])
        src_col = sb("src_col", [P, TILES])
        ident = sb("ident", [P, P])
        tri = sb("tri", [P, P])
        node_col = sb("node_col", [P, 1])
        cv_col = sb("cv_col", [P, 1])
        cu = sb("cu", [P, KU])
        dummy_col = sb("dummy_col", [P, 1])
        int_col = sb("int_col", [P, 2], I32)
        ones_bf = sb("ones_bf", [NPART, P], BF16)
        eps_col = sb("eps_col", [P, 1])
        ones_col = sb("ones_col", [P, 1])
        far_i = sb("far_i", [1, 1], I32)
        attr_n = sb("attr_n", [NP, EP, 2])
        src_m = sb("src_m", [P, EP], I32)
        dst_m = sb("dst_m", [P, EP], I32)
        src_n, dst_n = src_m[0:NP, :], dst_m[0:NP, :]
        src_f = sb("src_f", [NP, EP])
        r_n = sb("r_n", [NP, EP], BF16)
        rs_n = sb("rs_n", [NP, RP, 3 * RE], U8)
        parts_m = sb("parts_m", [P, 2 * EP], BF16)
        parts = parts_m[0:NP, 0:2 * NPART * RE].rearrange("p (s k e) -> p s k e", s=2, k=NPART)
        rest = sb("rest", [NP, 2, RE])
        base_i = sb("base_i", [NP, RP, 4], I32)
        base_f = sb("base_f", [NP, RP, 2])
        span = sb("span", [NP, 4])
        zero = sb("zero", [P, AR * FO // 4])
        w_sb = sb("w_sb", [P, KV, KU, FO])
        stat = sb("stat", [NP, 3, NN])
        YST = 2
        ZN = 2 * NN * F + YST * 4 * YROW
        zone = sb("zone", [P, ZN])
        x_n = zone[0:NP, 0:NN * F]
        sq_n = zone[0:NP, NN * F:2 * NN * F]
        h_t = zone[:, NN * F:NN * F + NBLK * NP].rearrange("p (b n) -> p b n", n=NP)
        y_st = zone[:, 2 * NN * F:].rearrange("p (s g c) -> p s g c", s=YST, g=4)
        CMAX = HT[0] * P
        used = [0]

        def carve(cols):
            a = zone[:, used[0]:used[0] + cols]
            used[0] += cols
            assert used[0] <= ZN
            return a

        rs = [carve(3 * RE // 4).bitcast(U8) for _ in range(2)]
        pick = [carve(CMAX) for _ in range(4)]
        same = [carve(CMAX) for _ in range(4)]
        prod = [carve(CMAX) for _ in range(2)]
        msg = [carve(HT[0] * FO) for _ in range(4)]
        summed = [carve(FO) for _ in range(2 * RT)]
        count = [carve(HT[0]) for _ in range(4)]
        moved = [carve(HT[0]) for _ in range(4)]
        row_idx = carve(2 * RT).bitcast(I32)
        shared = used[0]
        vrow = [carve(CMAX // 2).bitcast(BF16)[0:NPART, :] for _ in range(4)]
        win = [carve(IO) for _ in range(4)]
        dist = [carve(CMAX) for _ in range(2)]
        tent_v = [carve(CMAX) for _ in range(4)]
        used[0] = shared
        yg = [carve(HT[0] * YROW) for _ in range(2)]
        tent_g = [carve(HT[0] * KV) for _ in range(2)]
        minus_g = [carve(HT[0] * KV) for _ in range(2)]
        dst_idx = carve(4 * HT[0]).bitcast(I32)
        v_col = parts_m[:, :].bitcast(F32)[:, 0:TILES]
        dst_f = src_m[0:NP, :].bitcast(F32)
        dst_col = dst_m[:, 0:TILES].bitcast(F32)
        bank = [ctx.enter_context(nc.psum_tensor(f"bank{i}", [P, 512], F32)) for i in range(8)]

        def r_row(slot):
            a = slot % 2
            return rs[slot // 2][:, H0[a] * P:(H0[a] + HT[a]) * P]

        def src_row(slot, t):
            start = (H0[slot % 2] + t) * P
            return rs[slot // 2][:, RE:3 * RE].bitcast(U16)[:, start:start + P]

        ps_v = [bank[a][:, 0:HT[a] * P] for a in range(2)]
        ps_g = [bank[2 + a][:, 0:HT[a] * P] for a in range(2)]
        ps_m = [bank[4 + a][:, 0:HT[a] * FO] for a in range(2)]

        ld_x, ld_w, ld_src, ld_dst, ld_attr = (sem(f"ld_{n}") for n in ("x", "w", "src", "dst", "attr"))
        const_step, const_ready = sem("const_step"), sem("const_ready")
        ln_step, ln_done = sem("ln_step"), sem("ln_done")
        zero_ready = sem("zero_ready")
        src_cast = sem("src_cast")
        part_step, part_done = sem("part_step"), sem("part_done")
        part_out = [sem(f"part_out{i}") for i in range(2)]
        r_step, r_done, rs_cast, rs_out = sem("r_step"), sem("r_done"), sem("rs_cast"), sem("rs_out")
        base_done, base_out = sem("base_done"), sem("base_out")
        far_ps, far_ready = sem("far_ps"), sem("far_ready")
        col_ps, col_read = sem("col_ps"), sem("col_read")
        abs_u, tent_u_done = sem("abs_u"), sem("tent_u_done")
        ht_ps, ht_read = sem("ht_ps"), sem("ht_read")
        y_ps, y_copy_a, y_copy_v = sem("y_ps"), sem("y_copy_a"), sem("y_copy_v")
        y_out = [sem(f"y_out{i}") for i in range(YST)]
        s_vrow = [sem(f"v_rows_in{i}") for i in range(4)]
        s_rs = [sem(f"r_src_in{i}") for i in range(2)]
        s_win = [sem(f"window_in{i}") for i in range(4)]
        s_gat = [sem(f"gathered{i}") for i in range(2)]
        v_ps = sem("v_broadcast")
        g_ps, m_ps = sem("gather_product"), sem("message_sums")
        dist_done, tv_done = sem("dist_done"), sem("tent_v_done")
        pick_done, same_done = sem("pick_done"), sem("same_done")
        prod_done, msg_done = sem("prod_done"), sem("msg_done")
        moved_done, idx_done = sem("moved_done"), sem("idx_done")
        sum_out = sem("sum_copied")
        landed = [sem(f"landed{b}") for b in range(NACC)]
        col2_ps, col2_free, col2_read, dst_cast = (sem(n) for n in ("col2_ps", "col2_free", "col2_read", "dst_cast"))
        tg_step, yg_mult, yg_done = sem("tg_step"), sem("yg_mult"), sem("yg_done")
        didx_done = sem("didx_done")
        scatter_turn, gather_turn = sem("scatter_turn"), sem("gather_turn")
        fin_in = [sem(f"fin_in{b}") for b in range(NACC)]
        fin_add, fin_out = sem("fin_add"), sem("fin_out")
        START = [32] + [16] * (NACC - 1)

        half_cols = [slice(H0[a] * P, (H0[a] + HT[a]) * P) for a in range(2)]

        def run_steps(eng, step, lead, lag):
            head = 6
            first = head // 2
            end = ROUNDS - 2 - (ROUNDS - 2 - first) % 2
            for h in range(-lead, head):
                step(h, h % 4, h // 2)
            with eng.Fori(first, end - 1, 2) as i:
                q = eng.snap(i)
                for k in range(4):
                    step(2 * q + k, (2 * first + k) % 4, q + k // 2)
            for h in range(2 * end, LAST + lag + 1):
                step(h, h % 4, h // 2)

        def inside(h, d):
            return not isinstance(h, int) or 0 <= h + d <= LAST

        def wait_half(eng, s, h, per=1):
            if not isinstance(h, int) or h >= 0:
                eng.wait_ge(s, h * per + per)

        def wait_slot(eng, s, h, slot, ring):
            if isinstance(h, int):
                eng.wait_ge(s, 16 * (h // ring + 1))
            else:
                eng.wait_ge(s, h * (16 // ring) + (16 - (slot % ring) * (16 // ring)))

        def wait_rs(eng, q, slot):
            eng.wait_ge(s_rs[slot // 2], 16 * (q // 2 + 1) if isinstance(q, int) else q * 8 + (16 - 8 * (slot // 2)))

        def tiles_of(q, a):
            return q * RT + H0[a]

        def cut(ap, start, n):
            return ap[:, start:start + n] if isinstance(start, int) else ap[:, bass.ds(start, n)]

        def fin_buf(b):
            if b < 3:
                part = NN * F // KU
                return tent_u[0:NP, b * part:(b + 1) * part, :].rearrange("p t i -> p (t i)")
            part = NN * F // 2
            return attr_n[:, (b - 3) * part:(b - 2) * part, :].rearrange("p e c -> p (e c)")

        block = ctx.enter_context(nc.Block())

        @block.sync
        def _(sp):
            sp.dma_start(x_n, x.rearrange("(p n) f -> p (n f)", p=NP)).then_inc(ld_x, 16)
            sp.dma_start(src_n[:, :], src.rearrange("(p e) -> p e", p=NP)).then_inc(ld_src, 16)
            sp.dma_start(attr_n[:, :, :], attr.rearrange("(p e) c -> p e c", p=NP)).then_inc(ld_attr, 16)
            for g in range(4):
                for i in range(KU):
                    sp.dma_start(w_sb[g * F:(g + 1) * F, :, i, :],
                                 weight[i].rearrange("j f o -> f j o")).then_inc(ld_w, 16)
            sp.dma_start(dst_n[:, :], dst.rearrange("(p e) -> p e", p=NP)).then_inc(ld_dst, 16)
            sp.wait_ge(base_done, 1)
            sp.dma_start(base_d.rearrange("(p r) c -> p r c", p=NP), base_i[:, :, :]).then_inc(base_out, 16)
            sp.wait_ge(rs_cast, 2)
            sp.dma_start(rs_d.rearrange("(p r) c -> p r c", p=NP), rs_n[:, :, :]).then_inc(rs_out, 16)
            vrow_v = vrow_d.rearrange("k (p c e) -> p k c e", p=NP, c=RP)
            y_v = y_d.rearrange("(p n) c -> p n c", p=NP)

            def store_parts(c):
                sp.wait_ge(part_done, c + 1)
                sp.dma_start(vrow_v[:, :, c, :], parts[:, c % 2, :, :]).then_inc(part_out[c % 2], 16)

            def store_y(b):
                sp.wait_ge(y_copy_a, 2 * (b + 1))
                sp.wait_ge(y_copy_v, 2 * (b + 1))
                sp.dma_start(y_v[:, 4 * b:4 * b + 4, :], y_st[0:NP, b % YST, :, :]).then_inc(y_out[b % YST], 16)

            for b in range(NBLK):
                if b % 3 == 0 and b // 3 < RP:
                    store_parts(b // 3)
                store_y(b)

            sp.wait_ge(base_out, 16)
            sp.wait_ge(rs_out, 16)
            for i in range(2):
                sp.wait_ge(part_out[i], 16 * len(range(i, RP, 2)))
            for i in range(YST):
                sp.wait_ge(y_out[i], 16 * len(range(i, NBLK, YST)))
            sp.wait_ge(far_ready, 1)

            y_w = y_d.rearrange("n (j c) -> (n j) c", j=KV)

            def load_v(h, slot, q):
                start = tiles_of(q, slot % 2) * P
                cols = HT[slot % 2] * P
                wait_half(sp, v_ps, h - 4)
                sp.dma_start(vrow[slot][:, 0:cols], cut(vrow_d, start, cols)).then_inc(s_vrow[slot], 16)

            def window_step(base):
                def step(h, slot, q):
                    if inside(h, 2):
                        load_v(h + 2, (slot + 2) % 4, q + 1)
                    if not inside(h, 0):
                        return
                    a = slot % 2
                    if a == 0:
                        lines = [base_d[q:q + 1, i:i + 1] if isinstance(q, int) else base_d[bass.ds(q, 1), i:i + 1]
                                 for i in range(2)]
                        base[:] = [sp.value_load(line, min_val=0, max_val=N - WIN) for line in lines]
                    wait_half(sp, g_ps, h - 4)
                    sp.dma_start(win[slot], y_w[bass.ds(base[a] * KV, P), :]).then_inc(s_win[slot], 16)
                return step

            far = sp.value_load(far_i[0:1, 0:1], min_val=0, max_val=1)
            with sp.If(far == 0):
                run_steps(sp, window_step([None, None]), 2, 0)

            for b in range(NACC):
                sp.wait_ge(landed[b], START[b] + 16 * ROUNDS)
                dest = fin_buf(b)
                sp.dma_start(dest, acc_d[b][0:N, :].rearrange("(p n) f -> p (n f)", p=NP)).then_inc(fin_in[b], 16)
            sp.wait_ge(fin_add, NACC - 1)
            sp.dma_start(out.rearrange("(p n) f -> p (n f)", p=NP), fin_buf(0)).then_inc(fin_out, 16)
            sp.wait_ge(fin_out, 16)

        @block.gpsimd
        def _(pool):
            steps = [0]

            def chain(ins):
                ins.then_inc(const_step, 1)
                steps[0] += 1
                pool.wait_ge(const_step, steps[0])

            nc.gpsimd.memset(zero[:, :], 0.0).then_inc(zero_ready, 1)
            chain(nc.gpsimd.memset(ident[:, :], 0.0))
            chain(nc.gpsimd.affine_select(out=ident[:, :], in_=ident[:, :], compare_op=ALU.not_equal, fill=1.0,
                                          base=0, pattern=[[-1, P]], channel_multiplier=1))
            chain(nc.gpsimd.memset(tri[:, :], 1.0))
            chain(nc.gpsimd.affine_select(out=tri[:, :], in_=tri[:, :], compare_op=ALU.is_ge, fill=0.0,
                                          base=0, pattern=[[-1, P]], channel_multiplier=1))
            chain(nc.gpsimd.memset(ones_bf[:, :], 1.0))
            chain(nc.gpsimd.iota(int_col[:, 0:1], pattern=[[0, 1]], base=0, channel_multiplier=1))
            nc.gpsimd.tensor_scalar(dummy_col[:, :], int_col[:, 0:1], float(N), None, ALU.add).then_inc(const_ready, 1)

            pool.dma_start(acc_d[0][0:N, :].rearrange("(p n) f -> p (n f)", p=NP),
                         x.rearrange("(p n) f -> p (n f)", p=NP)).then_inc(landed[0], 16)
            pool.wait_ge(zero_ready, 1)
            rest_rows = AROWS - N
            zp = max(d for d in range(1, P + 1) if rest_rows % d == 0)
            pool.dma_start(acc_d[0][N:AROWS, :].rearrange("(p n) f -> p (n f)", p=zp),
                         zero[0:zp, 0:rest_rows // zp * FO]).then_inc(landed[0], 16)
            zsrc = zero[:, :].unsqueeze(1).to_broadcast([P, 4, AR * FO // 4])
            for b in range(1, NACC):
                pool.dma_start(acc_d[b].rearrange("(p k n) f -> p k (n f)", p=P, k=4), zsrc)\
                  .then_inc(landed[b], 16)
            pool.wait_ge(r_done, 1)
            nc.gpsimd.tensor_copy(rs_n[:, :, 0:RE], r_n[:, :].rearrange("p (r e) -> p r e", r=RP)).then_inc(rs_cast, 1)
            pool.wait_ge(ld_attr, 16)
            n = [0]

            def link(ins):
                ins.then_inc(part_step, 1)
                n[0] += 1
                pool.wait_ge(part_step, n[0])

            for c in range(RP):
                s = c % 2
                if c >= 2:
                    pool.wait_ge(part_out[s], 16 * (c // 2))
                e = slice(c * RE, (c + 1) * RE)
                v = attr_n[:, e, 1]
                link(nc.gpsimd.tensor_copy(parts[:, s, 0, :], v))
                link(nc.gpsimd.tensor_tensor(rest[:, 0, :], v, parts[:, s, 0, :], ALU.subtract))
                link(nc.gpsimd.tensor_copy(parts[:, s, 1, :], rest[:, 0, :]))
                nc.gpsimd.tensor_tensor(parts[:, s, 2, :], rest[:, 0, :], parts[:, s, 1, :], ALU.subtract)\
                  .then_inc(part_done, 1)
                pool.wait_ge(part_done, c + 1)

            for i in range(YST):
                pool.wait_ge(y_out[i], 16 * len(range(i, NBLK, YST)))
            pool.wait_ge(far_ready, 1)

            def scatter(h, slot, q):
                a = slot % 2
                wait_half(pool, sum_out, h)
                wait_half(pool, idx_done, h)
                for b in range(H0[a], H0[a] + HT[a]):
                    pool.wait_ge(landed[b], q * 16 + START[b])
                pool.sem_inc(scatter_turn, 1)
                for t in range(HT[a]):
                    b = H0[a] + t
                    k = (slot // 2) * RT + b
                    idx = row_idx[:, k:k + 1]
                    pool.indirect_dma_start(acc_d[b], bass.IndirectOffsetOnAxis(ap=idx, axis=0),
                                            summed[k], None,
                                            compute_op=ALU.add).then_inc(landed[b], 16)

            def gather_scatter(h, slot, q):
                if inside(h, 2):
                    a = slot % 2
                    slot2 = (slot + 2) % 4
                    wait_half(pool, yg_done, h)
                    wait_half(pool, didx_done, h + 2)
                    pool.sem_inc(gather_turn, 1)
                    for t in range(HT[a]):
                        k = slot2 * HT[0] + t
                        idx = dst_idx[:, k:k + 1]
                        pool.indirect_dma_start(yg[a][:, t * YROW:(t + 1) * YROW], None, y_d,
                                                bass.IndirectOffsetOnAxis(ap=idx, axis=0)).then_inc(s_gat[a], 16)
                if inside(h, 0):
                    scatter(h, slot, q)

            far = pool.value_load(far_i[0:1, 0:1], min_val=0, max_val=1)
            with pool.If(far == 0):
                run_steps(pool, scatter, 0, 0)
            with pool.Else():
                run_steps(pool, gather_scatter, 2, 0)

        NCB = -(-TP // 4)

        def columns(c):
            m = min(4, TP - 4 * c)
            return m

        @block.scalar
        def _(act):
            act.wait_ge(ld_src, 16)
            nc.scalar.copy(src_f[:, :], src_n[:, :]).then_inc(src_cast, 1)
            nc.scalar.copy(rs_n[:, :, RE:3 * RE].bitcast(U16), src_n[:, :].rearrange("p (r e) -> p r e", r=RP))\
              .then_inc(rs_cast, 1)
            act.wait_ge(const_ready, 2)
            for c in range(NCB):
                m = columns(c)
                act.wait_ge(col_ps, 2 * c + 1)
                dest = src_col[:, :].rearrange("p (a k) -> p k a", k=TP)[:, 4 * c:4 * c + m, :]
                nc.scalar.copy(dest, bank[6][:, 0:m * NP].rearrange("p (k a) -> p k a", k=m)).then_inc(col_read, 1)
                act.wait_ge(col_ps, 2 * c + 2)
                for i in range(KU):
                    dest = tent_u[:, :, i].rearrange("p (a k) -> p k a", k=TP)[:, 4 * c:4 * c + m, :]
                    last = nc.scalar.activation(dest, bank[7][:, 0:m * NP].rearrange("p (k a) -> p k a", k=m),
                                                ACT.Abs, bias=cu[:, i:i + 1], scale=1.0)
                last.then_inc(col_read, 1)
            act.wait_ge(col_read, 2 * NCB)
            flat = tent_u[:, :, :].rearrange("p t i -> p (t i)")
            nc.scalar.activation(flat, flat, ACT.Relu, bias=ones_col[:, :], scale=-SLOPE).then_inc(tent_u_done, 1)
            act.wait_ge(ln_step, 3)
            nc.scalar.activation(sq_n, x_n, ACT.Square).then_inc(ln_step, 1)
            act.wait_ge(ln_step, 5)
            nc.scalar.activation(stat[:, 1, :], stat[:, 2, :], ACT.Sqrt, bias=eps_col[0:NP, :], scale=1.0 / F)\
              .then_inc(ln_step, 1)
            for b in range(NBLK):
                if b >= YST:
                    act.wait_ge(y_out[b % YST], 16 * (b // YST))
                for g in (1, 3):
                    act.wait_ge(y_ps, 4 * b + g + 1)
                    nc.scalar.copy(y_st[0:NP, b % YST, g, :], bank[2 + g][0:NP, :]).then_inc(y_copy_a, 1)
            for i in range(YST):
                act.wait_ge(y_out[i], 16 * len(range(i, NBLK, YST)))
            act.wait_ge(far_ready, 1)

            def load_rs(h, slot, q):
                line = rs_d[q:q + 1, :] if isinstance(q, int) else rs_d[bass.ds(q, 1), :]
                wait_half(act, same_done, h - 3)
                act.dma_start(rs[slot // 2], line.to_broadcast([P, 3 * RE])).then_inc(s_rs[slot // 2], 16)

            def tents(h, slot):
                a = slot % 2
                cols = HT[a] * P
                wait_half(act, v_ps, h)
                wait_half(act, tv_done, h - 2)
                nc.scalar.activation(dist[a][:, 0:cols], ps_v[a], ACT.Abs, bias=cv_col[:, :], scale=1.0)\
                  .then_inc(dist_done, 1)
                wait_half(act, pick_done, h - 4)
                wait_half(act, dist_done, h)
                nc.scalar.activation(tent_v[slot][:, 0:cols], dist[a][:, 0:cols], ACT.Relu,
                                     bias=ones_col[:, :], scale=-SLOPE).then_inc(tv_done, 1)

            def copy_sums(h, slot, q):
                a = slot % 2
                wait_half(act, m_ps, h)
                if not isinstance(h, int) or h >= 4:
                    for b in range(H0[a], H0[a] + HT[a]):
                        act.wait_ge(landed[b], q * 16 + START[b] - 16)
                for t in range(HT[a]):
                    ins = nc.scalar.copy(summed[(slot // 2) * RT + H0[a] + t], ps_m[a][:, t * FO:(t + 1) * FO])
                ins.then_inc(sum_out, 1)

            def step(h, slot, q, windows=True):
                if inside(h, -3):
                    copy_sums(h - 3, (slot - 3) % 4, q - 2 + slot % 2)
                if windows and inside(h, 2):
                    tents(h + 2, (slot + 2) % 4)
                if slot % 2 == 0 and inside(h, 2):
                    load_rs(h + 2, (slot + 2) % 4, q + 1)

            far = act.value_load(far_i[0:1, 0:1], min_val=0, max_val=1)
            with act.If(far == 0):
                run_steps(act, step, 2, 3)
            with act.Else():
                run_steps(act, lambda h, slot, q: step(h, slot, q, False), 2, 3)

        @block.vector
        def _(dve):
            nc.vector.memset(ones_col[:, :], 1.0)
            nc.vector.memset(eps_col[:, :], EPS)
            for i in range(KU):
                last = nc.vector.memset(cu[:, i:i + 1], 1.0 - 2.0 * i / (KU - 1))
            last.then_inc(const_ready, 1)
            dve.wait_ge(ld_x, 16)
            x3 = x_n.rearrange("p (n f) -> p n f", f=F)
            sq3 = sq_n.rearrange("p (n f) -> p n f", f=F)
            wide = [NP, NN, F]
            nc.vector.tensor_reduce(stat[:, 0, :], x3, AX.X, ALU.add).then_inc(ln_step, 1)
            dve.wait_ge(ln_step, 1)
            nc.vector.tensor_scalar(stat[:, 1, :], stat[:, 0, :], 1.0 / F, None, ALU.mult).then_inc(ln_step, 1)
            dve.wait_ge(ln_step, 2)
            nc.vector.tensor_tensor(x3, x3, stat[:, 1, :].unsqueeze(2).to_broadcast(wide), ALU.subtract)\
              .then_inc(ln_step, 1)
            dve.wait_ge(ln_step, 4)
            nc.vector.tensor_reduce(stat[:, 2, :], sq3, AX.X, ALU.add).then_inc(ln_step, 1)
            dve.wait_ge(ln_step, 6)
            nc.vector.reciprocal(stat[:, 0, :], stat[:, 1, :]).then_inc(ln_step, 1)
            dve.wait_ge(ln_step, 7)
            nc.vector.scalar_tensor_tensor(out=x3, in0=x3, scalar=0.0,
                                           in1=stat[:, 0, :].unsqueeze(2).to_broadcast(wide),
                                           op0=ALU.max, op1=ALU.mult).then_inc(ln_done, 1)
            dve.wait_ge(const_ready, 2)
            nc.vector.tensor_scalar(int_col[:, 1:2], int_col[:, 0:1], 2, None, ALU.arith_shift_right)\
              .then_inc(r_step, 1)
            dve.wait_ge(r_step, 1)
            nc.vector.tensor_copy(node_col[:, :], int_col[:, 1:2]).then_inc(r_step, 1)
            dve.wait_ge(r_step, 2)
            nc.vector.tensor_scalar(int_col[:, 1:2], int_col[:, 0:1], KV - 1, None, ALU.bitwise_and)\
              .then_inc(r_step, 1)
            dve.wait_ge(r_step, 3)
            nc.vector.tensor_scalar(cv_col[:, :], int_col[:, 1:2], -2.0 / (KV - 1), 1.0, ALU.mult, ALU.add)\
              .then_inc(r_step, 1)
            dve.wait_ge(ld_dst, 16)
            d5 = dst_n[:, :].rearrange("p (r t e) -> p r t e", r=RP, t=RT)
            nc.vector.memset(base_i[:, :, :], 0).then_inc(r_step, 1)
            dve.wait_ge(r_step, 5)
            for a in range(2):
                nc.vector.tensor_scalar(base_f[:, :, a], d5[:, :, H0[a], 0], float(N - WIN), None, ALU.min)
                last = nc.vector.tensor_scalar(base_i[:, :, a], d5[:, :, H0[a], 0], float(N - WIN), None, ALU.min)
            last.then_inc(base_done, 1)
            dve.wait_ge(base_done, 1)
            dr = dst_n[:, :].rearrange("p (r c) -> p r c", r=RP)
            rr = r_n[:, :].rearrange("p (r c) -> p r c", r=RP)
            for a in range(2):
                last = nc.vector.tensor_tensor(rr[:, :, half_cols[a]], dr[:, :, half_cols[a]],
                                               base_f[:, :, a:a + 1].to_broadcast([NP, RP, HT[a] * P]), ALU.subtract)
            last.then_inc(r_done, 1)
            dve.wait_ge(r_done, 1)
            nc.vector.tensor_reduce(span[:, 0:1], r_n[:, :], AX.X, ALU.min)
            nc.vector.tensor_reduce(span[:, 1:2], r_n[:, :], AX.X, ALU.max).then_inc(r_step, 1)
            dve.wait_ge(r_step, 6)
            nc.vector.tensor_scalar(span[:, 0:1], span[:, 0:1], 0.0, None, ALU.is_lt)
            nc.vector.tensor_scalar(span[:, 1:2], span[:, 1:2], float(WIN - 1), None, ALU.is_gt).then_inc(r_step, 1)
            dve.wait_ge(r_step, 7)
            nc.vector.tensor_tensor(span[:, 2:3], span[:, 0:1], span[:, 1:2], ALU.add).then_inc(r_step, 1)
            for b in range(NBLK + 1):
                if b < NBLK:
                    dve.wait_ge(ht_ps, b + 1)
                    nc.vector.tensor_copy(h_t[:, b, :], bank[b % 2][:, 0:NP]).then_inc(ht_read, 1)
                if b >= 1:
                    c = b - 1
                    if c >= YST:
                        dve.wait_ge(y_out[c % YST], 16 * (c // YST))
                    for g in (0, 2):
                        dve.wait_ge(y_ps, 4 * c + g + 1)
                        nc.vector.tensor_copy(y_st[0:NP, c % YST, g, :], bank[2 + g][0:NP, :]).then_inc(y_copy_v, 1)
            dve.wait_ge(far_ps, 1)
            nc.vector.tensor_scalar(far_i[0:1, 0:1], bank[0][0:1, 0:1], 1.0, None, ALU.min).then_inc(far_ready, 1)
            dve.wait_ge(far_ready, 1)
            for i in range(YST):
                dve.wait_ge(y_out[i], 16 * len(range(i, NBLK, YST)))
            dve.wait_ge(tent_u_done, 1)
            dve.wait_ge(part_done, RP)

            def build_pick(h, slot, q):
                a = slot % 2
                cols = HT[a] * P
                wait_rs(dve, q, slot)
                wait_half(dve, tv_done, h)
                wait_half(dve, g_ps, h - 4)
                nc.vector.scalar_tensor_tensor(out=pick[slot][:, 0:cols], in0=r_row(slot), scalar=node_col[:, :],
                                               in1=tent_v[slot][:, 0:cols], op0=ALU.is_equal, op1=ALU.mult)\
                  .then_inc(pick_done, 1)

            def build_same(h, slot, q):
                a = slot % 2
                wait_rs(dve, q, slot)
                wait_half(dve, m_ps, h - 4)
                wait_half(dve, moved_done, h - 4)
                for t in range(HT[a]):
                    ins = nc.vector.scalar_tensor_tensor(
                        out=same[slot][:, t * P:(t + 1) * P], in0=src_row(slot, t),
                        scalar=cut(src_col, tiles_of(q, a) + t, 1), in1=tri[:, :],
                        op0=ALU.is_equal, op1=ALU.mult, accum_out=count[slot][:, t:t + 1])
                ins.then_inc(same_done, 1)

            def weigh(h, slot, q):
                a = slot % 2
                n = HT[a]
                if far_form[0]:
                    g_in = pick[slot][:, 0:n * P]
                    wait_half(dve, yg_done, h)
                else:
                    g_in = ps_g[a]
                    wait_half(dve, g_ps, h)
                wait_half(dve, msg_done, h - 2)
                tu = cut(tent_u, tiles_of(q, a), n).rearrange("p t i -> p (t i)")
                nc.vector.tensor_tensor(prod[a][:, 0:n * IO].rearrange("p (k o) -> p k o", o=FO),
                                        g_in.rearrange("p (k o) -> p k o", o=FO),
                                        tu.unsqueeze(2).to_broadcast([P, n * KU, FO]), ALU.mult).then_inc(prod_done, 1)

            def sum_i(h, slot):
                a = slot % 2
                n = HT[a]
                wait_half(dve, prod_done, h)
                wait_half(dve, m_ps, h - 4)
                nc.vector.tensor_reduce(msg[slot][:, 0:n * FO].rearrange("p (t o) -> p t o", o=FO),
                                        prod[a][:, 0:n * IO].rearrange("p (t i o) -> p t o i", t=n, i=KU),
                                        AX.X, ALU.add).then_inc(msg_done, 1)

            def mark_repeats(h, slot):
                a = slot % 2
                n = HT[a]
                wait_half(dve, same_done, h)
                wait_half(dve, idx_done, h - 4)
                nc.vector.scalar_tensor_tensor(out=moved[slot][:, 0:n], in0=count[slot][:, 0:n], scalar=1.0,
                                               in1=dummy_col[:, :].to_broadcast([P, n]),
                                               op0=ALU.is_gt, op1=ALU.mult).then_inc(moved_done, 1)

            def choose_rows(h, slot, q):
                a = slot % 2
                n = HT[a]
                wait_half(dve, moved_done, h)
                t0 = tiles_of(q, a)
                if not isinstance(h, int) or h >= 4:
                    for b in range(H0[a], H0[a] + n):
                        dve.wait_ge(landed[b], q * 16 + START[b] - 16)
                k = (slot // 2) * RT + H0[a]
                nc.vector.tensor_tensor(row_idx[:, k:k + n], moved[slot][:, 0:n], cut(src_col, t0, n), ALU.max)\
                  .then_inc(idx_done, 1)

            far_form = [False]

            def combine(h, slot, q):
                a = slot % 2
                n = HT[a]
                tg = tent_g[a][:, 0:n * KV].rearrange("p (t j) -> p t j", j=KV)
                wait_half(dve, yg_done, h - 2)
                nc.vector.tensor_tensor(tg, cut(v_col, tiles_of(q, a), n).unsqueeze(2).to_broadcast([P, n, KV]),
                                        cu[:, :].unsqueeze(1).to_broadcast([P, n, KV]), ALU.add).then_inc(tg_step, 1)
                dve.wait_ge(tg_step, h * 4 + 1)
                flat = tent_g[a][:, 0:n * KV]
                nc.vector.tensor_scalar(minus_g[a][:, 0:n * KV], flat, -1.0, None, ALU.mult).then_inc(tg_step, 1)
                dve.wait_ge(tg_step, h * 4 + 2)
                nc.vector.tensor_tensor(flat, flat, minus_g[a][:, 0:n * KV], ALU.max).then_inc(tg_step, 1)
                dve.wait_ge(tg_step, h * 4 + 3)
                nc.vector.tensor_scalar(flat, flat, -SLOPE, 1.0, ALU.mult, ALU.add).then_inc(tg_step, 1)
                dve.wait_ge(tg_step, h * 4 + 4)
                dve.wait_ge(s_gat[a], q * (16 * n) + 16 * n)
                y4 = yg[a][:, 0:n * YROW].rearrange("p (k c) -> p k c", c=IO)
                nc.vector.scalar_tensor_tensor(out=y4, in0=flat.unsqueeze(2).to_broadcast([P, n * KV, IO]), scalar=0.0,
                                               in1=y4, op0=ALU.max, op1=ALU.mult).then_inc(yg_mult, 1)
                wait_half(dve, yg_mult, h)
                for t in range(n):
                    ins = nc.vector.tensor_reduce(pick[slot][:, t * P:(t + 1) * P],
                                                  yg[a][:, t * YROW:(t + 1) * YROW].rearrange("p (j c) -> p c j", j=KV),
                                                  AX.X, ALU.add)
                ins.then_inc(yg_done, 1)

            def index_dst(h, slot, q):
                a = slot % 2
                wait_half(dve, yg_mult, h - 4)
                nc.vector.tensor_copy(dst_idx[:, slot * HT[0]:slot * HT[0] + HT[a]],
                                      cut(dst_col, tiles_of(q, a), HT[a])).then_inc(didx_done, 1)

            def step(h, slot, q):
                if inside(h, -2):
                    weigh(h - 2, (slot - 2) % 4, q - 1)
                if inside(h, 0):
                    if far_form[0]:
                        combine(h, slot, q)
                    else:
                        build_pick(h, slot, q)
                if inside(h, -2):
                    sum_i(h - 2, (slot - 2) % 4)
                if far_form[0] and inside(h, 4):
                    index_dst(h + 4, slot, q + 2)
                if inside(h, -3):
                    mark_repeats(h - 3, (slot - 3) % 4)
                if inside(h, 0):
                    build_same(h, slot, q)
                if inside(h, -3):
                    choose_rows(h - 3, (slot - 3) % 4, q - 2 + slot % 2)

            far = dve.value_load(far_i[0:1, 0:1], min_val=0, max_val=1)
            with dve.If(far == 0):
                run_steps(dve, step, 0, 3)
            with dve.Else():
                far_form[0] = True
                nc.vector.tensor_copy(dst_f, dst_n[:, :]).then_inc(dst_cast, 1)
                for c in range(NCB):
                    m = columns(c)
                    dve.wait_ge(col2_ps, c + 1)
                    for k, dest in enumerate((dst_col, v_col)):
                        last = nc.vector.tensor_copy(
                            dest.rearrange("p (a k) -> p k a", k=TP)[:, 4 * c:4 * c + m, :],
                            bank[6 + k][:, 0:m * NP].rearrange("p (k a) -> p k a", k=m))
                    if c < NCB - 1:
                        last.then_inc(col2_free, 1)
                    else:
                        last.then_inc(col2_read, 1)
                dve.wait_ge(col2_read, 1)
                run_steps(dve, step, 4, 3)

            dve.wait_ge(fin_in[0], 16)
            for b in range(1, NACC):
                dve.wait_ge(fin_in[b], 16)
                if b >= 2:
                    dve.wait_ge(fin_add, b - 1)
                nc.vector.tensor_tensor(fin_buf(0), fin_buf(0), fin_buf(b), ALU.add).then_inc(fin_add, 1)

        @block.tensor
        def _(pe):
            idn = ident[0:NP, 0:NP]
            pe.wait_ge(const_ready, 2)
            pe.wait_ge(src_cast, 1)
            pe.wait_ge(ld_attr, 16)
            for c in range(NCB):
                m = columns(c)
                for k in range(2):
                    if c >= 1:
                        pe.wait_ge(col_read, 2 * c - 1 + k)
                    for t in range(m):
                        e = slice((4 * c + t) * P, (4 * c + t + 1) * P)
                        ins = nc.tensor.transpose(bank[6 + k][:, t * NP:(t + 1) * NP],
                                                  src_f[:, e] if k == 0 else attr_n[:, e, 0], idn)
                    ins.then_inc(col_ps, 1)
            pe.wait_ge(ln_done, 1)
            pe.wait_ge(ld_w, 16 * 4 * KU)

            def turn(b):
                if b >= 2:
                    pe.wait_ge(ht_read, b - 1)
                nc.tensor.transpose(bank[b % 2][:, 0:NP], x_n[:, b * P:(b + 1) * P], idn).then_inc(ht_ps, 1)

            turn(0)
            for b in range(NBLK):
                if b + 1 < NBLK:
                    turn(b + 1)
                pe.wait_ge(ht_read, b + 1)
                for g in range(4):
                    if b >= 1:
                        pe.wait_ge((y_copy_v, y_copy_a)[g % 2], 2 * (b - 1) + g // 2 + 1)
                    nc.tensor.matmul(bank[2 + g][0:NP, :], h_t[g * F:(g + 1) * F, b, :],
                                     w_sb[g * F:(g + 1) * F, :, :, :].rearrange("p j i o -> p (j i o)"),
                                     start=True, stop=True, tile_position=(g * F, 0)).then_inc(y_ps, 1)
            pe.wait_ge(r_step, 8)
            pe.wait_ge(ht_read, NBLK)
            nc.tensor.matmul(bank[0][0:1, 0:1], span[:, 2:3], ones_col[0:NP, :], start=True, stop=True)\
              .then_inc(far_ps, 1)
            pe.wait_ge(far_ready, 1)
            pe.wait_ge(y_copy_a, 2 * NBLK)
            pe.wait_ge(y_copy_v, 2 * NBLK)
            pe.wait_ge(col_read, 2 * NCB)

            def broadcast_v(h, slot):
                a = slot % 2
                wait_slot(pe, s_vrow[slot], h, slot, 4)
                wait_half(pe, dist_done, h - 2)
                nc.tensor.matmul(ps_v[a], ones_bf[:, :], vrow[slot][:, 0:HT[a] * P], start=True, stop=True)\
                  .then_inc(v_ps, 1)

            def gather(h, slot):
                a = slot % 2
                wait_half(pe, pick_done, h)
                wait_slot(pe, s_win[slot], h, slot, 4)
                wait_half(pe, prod_done, h - 2)
                for t in range(HT[a]):
                    ins = nc.tensor.matmul(ps_g[a][:, t * P:(t + 1) * P], pick[slot][:, t * P:(t + 1) * P],
                                           win[slot], start=True, stop=True)
                ins.then_inc(g_ps, 1)

            def sum_same(h, slot):
                a = slot % 2
                wait_half(pe, same_done, h)
                wait_half(pe, msg_done, h)
                wait_half(pe, sum_out, h - 2)
                for t in range(HT[a]):
                    ins = nc.tensor.matmul(ps_m[a][:, t * FO:(t + 1) * FO], same[slot][:, t * P:(t + 1) * P],
                                           msg[slot][:, t * FO:(t + 1) * FO], start=True, stop=True)
                ins.then_inc(m_ps, 1)

            def step(h, slot, q, windows=True):
                if windows and inside(h, 2):
                    broadcast_v(h + 2, (slot + 2) % 4)
                if windows and inside(h, 0):
                    gather(h, slot)
                if inside(h, -2):
                    sum_same(h - 2, (slot - 2) % 4)

            far = pe.value_load(far_i[0:1, 0:1], min_val=0, max_val=1)
            with pe.If(far == 0):
                run_steps(pe, step, 2, 2)
            with pe.Else():
                pe.wait_ge(dst_cast, 1)
                for c in range(NCB):
                    m = columns(c)
                    if c >= 1:
                        pe.wait_ge(col2_free, c)
                    for k in range(2):
                        for t in range(m):
                            e = slice((4 * c + t) * P, (4 * c + t + 1) * P)
                            ins = nc.tensor.transpose(bank[6 + k][:, t * NP:(t + 1) * NP],
                                                      dst_f[:, e] if k == 0 else attr_n[:, e, 1], idn)
                    ins.then_inc(col2_ps, 1)
                pe.wait_ge(col2_read, 1)
                run_steps(pe, lambda h, slot, q: step(h, slot, q, False), 0, 2)


_INS = ["x", "src", "dst", "edge_attr_2", "L0_gnn_weight"]


def kernel(**inputs):
    import concourse.bacc as _bacc
    from concourse.bass_utils import run_bass_kernel_spmd as _run

    nc = _bacc.Bacc("TRN2", target_bir_lowering=False, num_devices=1)
    arrays, args = {}, []
    for name in _INS:
        a = np.ascontiguousarray(inputs[name])
        arrays[f"in_{name}"] = a
        args.append(nc.dram_tensor(f"in_{name}", a.shape, mybir.dt.from_np(a.dtype), kind="ExternalInput").ap())
    shape = inputs["x"].shape
    args.append(nc.dram_tensor("out_x", shape, F32, kind="ExternalOutput").ap())
    edge_conv_kernel(nc, *args)
    r = _run(nc, [arrays], core_ids=[0])
    return r.results[0]["out_x"]
```

```python
from contextlib import ExitStack

import numpy as np

import concourse.bass as bass
from concourse import mybir

F32 = mybir.dt.float32
BF16 = mybir.dt.bfloat16
I32 = mybir.dt.int32
U8 = mybir.dt.uint8
U16 = mybir.dt.uint16
ALU = mybir.AluOpType
ACT = mybir.ActivationFunctionType
AX = mybir.AxisListType

P = 128
EPS = 1e-5


def edge_conv_kernel(nc, x, src, dst, attr, weight, out):
    N, F = x.shape
    E = src.shape[0]
    KU, KV, _, FO = weight.shape
    IO = KU * FO
    JF = KV * F
    assert JF == P
    NPART = 3
    WIN = 32
    WR = WIN * NPART
    SLOPE = (KU - 1) / 2.0
    TILES = E // P
    HT = (3, 2)
    H0 = (0, 3)
    RT = sum(HT)
    ROUNDS = TILES // RT
    HALVES = 2 * ROUNDS
    RE = RT * P
    NP = 125
    EP = E // NP
    RP = EP // RE
    TP = EP // P
    NN = N // NP
    NACC = RT
    AROWS = -(-(N + P) // (4 * P)) * 4 * P
    AR = AROWS // P
    assert E == ROUNDS * RE and EP == RP * RE and N == NP * NN and NN % 4 == 0
    LAST = HALVES - 1

    ctx = ExitStack()
    with ctx:
        def sb(name, shape, dt=F32):
            return ctx.enter_context(nc.sbuf_tensor(name, shape, dt))

        def sem(name):
            return ctx.enter_context(nc.semaphore(name))

        def dram(name, shape, dt=F32):
            return nc.dram_tensor(name, shape, dt, kind="Internal").ap()

        hp_d = dram("h_parts", (N, NPART * F), BF16)
        h_d = dram("h_rows", (N, F))
        vrow_d = dram("v_parts", (NPART, E), BF16)
        rs_d = dram("r_and_src", (ROUNDS, 3 * RE), U8)
        base_d = dram("window_base", (1, HALVES), I32)
        acc_d = [dram(f"accumulator_{b}", (AROWS, FO)) for b in range(NACC)]

        tent_u = sb("tent_u", [P, TILES, KU])
        src_col = sb("src_col", [P, TILES])
        ident = sb("ident", [P, P])
        tri = sb("tri", [P, P])
        node_col = sb("node_col", [P, 1])
        cv_col = sb("cv_col", [P, 1])
        cu = sb("cu", [P, KU])
        dummy_col = sb("dummy_col", [P, 1])
        int_col = sb("int_col", [P, 4], I32)
        ones_bf = sb("ones_bf", [NPART, P], BF16)
        eps_col = sb("eps_col", [P, 1])
        ones_col = sb("ones_col", [P, 1])
        far_i = sb("far_i", [1, 1], I32)
        attr_n = sb("attr_n", [NP, EP, 2])
        src_m = sb("src_m", [P, EP], I32)
        dst_m = sb("dst_m", [P, EP], I32)
        src_n, dst_n = src_m[0:NP, :], dst_m[0:NP, :]
        src_f = sb("src_f", [NP, EP])
        r_n = sb("r_n", [NP, EP], BF16)
        base_row = r_n[0:1, :].bitcast(I32)[:, 0:HALVES]
        rs_n = sb("rs_n", [NP, RP, 3 * RE], U8)
        parts_m = sb("parts_m", [P, 2 * EP], BF16)
        parts = parts_m[0:NP, 0:2 * NPART * RE].rearrange("p (s k e) -> p s k e", s=2, k=NPART)
        rest_p = sb("rest_p", [NP, RE])
        rest_v = sb("rest_v", [NP, RE])
        PC = 3
        base_i = sb("base_i", [NP, RP, 2], I32)
        base_f = sb("base_f", [NP, RP, 2])
        span = sb("span", [NP, 4])
        zero = sb("zero", [P, AR * FO // 4])
        w_sb = sb("w_sb", [P, KU, FO])
        stat = sb("stat", [NP, 3, NN])
        ZN = 2 * NN * F + NN * NPART * F // 2
        zone = sb("zone", [P, ZN])
        x_n = zone[0:NP, 0:NN * F]
        sq_n = zone[0:NP, NN * F:2 * NN * F]
        h_parts = zone[0:NP, 2 * NN * F:].bitcast(BF16).rearrange("p (n k f) -> p n k f", k=NPART, f=F)
        CMAX = HT[0] * P
        used = [0]

        def carve(cols):
            a = zone[:, used[0]:used[0] + cols]
            used[0] += cols
            assert used[0] <= ZN
            return a

        rs = [carve(3 * CMAX // 4).bitcast(U8) for _ in range(4)]
        gv = [carve(CMAX) for _ in range(4)]
        same = [carve(CMAX) for _ in range(4)]
        prod = [carve(CMAX) for _ in range(2)]
        msg = [carve(HT[0] * FO) for _ in range(4)]
        summed = [carve(FO) for _ in range(2 * RT)]
        count = [carve(HT[0]) for _ in range(4)]
        moved = [carve(HT[0]) for _ in range(4)]
        row_idx = carve(2 * RT).bitcast(I32)
        shared = used[0]
        vrow = [carve(CMAX // 2).bitcast(BF16)[0:NPART, :] for _ in range(4)]
        win = [carve(JF // 2).bitcast(BF16)[0:WR, :] for _ in range(4)]
        pick = [carve(CMAX // 2).bitcast(BF16)[0:WR, :] for _ in range(4)]
        dist = [carve(CMAX) for _ in range(2)]
        tent_v = [carve(CMAX) for _ in range(4)]
        used[0] = shared
        hg = [carve(HT[0] * F) for _ in range(2)]
        hv = [carve(CMAX) for _ in range(2)]
        tent_g = [carve(HT[0] * KV) for _ in range(2)]
        minus_g = [carve(HT[0] * KV) for _ in range(2)]
        dst_idx = carve(4 * HT[0]).bitcast(I32)
        v_col = parts_m[:, :].bitcast(F32)[:, 0:TILES]
        dst_f = src_m[0:NP, :].bitcast(F32)
        dst_col = dst_m[:, 0:TILES].bitcast(F32)
        bank = [ctx.enter_context(nc.psum_tensor(f"bank{i}", [P, 512], F32)) for i in range(8)]

        def r_row(slot):
            a = slot % 2
            return rs[slot][0:WR, 0:HT[a] * P]

        def src_row(slot, t):
            cols = HT[slot % 2] * P
            return rs[slot][:, cols:3 * cols].bitcast(U16)[:, t * P:(t + 1) * P]

        ps_v = [bank[a][:, 0:HT[a] * P] for a in range(2)]
        ps_g = [bank[2 + a][:, 0:HT[a] * P] for a in range(2)]
        ps_h = [bank[6 + a][:, 0:HT[a] * P] for a in range(2)]
        ps_m = [bank[4 + a][:, 0:HT[a] * FO] for a in range(2)]

        ld_x, ld_w, ld_src, ld_dst, ld_attr = (sem(f"ld_{n}") for n in ("x", "w", "src", "dst", "attr"))
        const_step, const_ready = sem("const_step"), sem("const_ready")
        ln_step, ln_done = sem("ln_step"), sem("ln_done")
        zero_ready = sem("zero_ready")
        src_cast = sem("src_cast")
        part_step, part_step_v = sem("part_step"), sem("part_step_v")
        part_done, part_done_v = sem("part_done"), sem("part_done_v")
        part_out = [sem(f"part_out{i}") for i in range(2)]
        r_step, r_done, rs_cast, rs_out = sem("r_step"), sem("r_done"), sem("rs_cast"), sem("rs_out")
        base_done, base_out, base_in = sem("base_done"), sem("base_out"), sem("base_in")
        far_ps, far_ready = sem("far_ps"), sem("far_ready")
        col_ps, col_read = sem("col_ps"), sem("col_read")
        abs_u, tent_u_done = sem("abs_u"), sem("tent_u_done")
        hp_step, hp_done, hp_out, h_out = sem("hp_step"), sem("hp_done"), sem("hp_out"), sem("h_out")
        s_vrow = [sem(f"v_rows_in{i}") for i in range(4)]
        s_rs = [sem(f"r_src_in{i}") for i in range(4)]
        s_win = [sem(f"window_in{i}") for i in range(4)]
        s_gat = [sem(f"gathered{i}") for i in range(2)]
        v_ps = sem("v_broadcast")
        g_ps, m_ps = sem("gather_product"), sem("message_sums")
        dist_done, tv_done = sem("dist_done"), sem("tent_v_done")
        h_ps, gv_done = sem("dst_rows"), sem("g_done")
        pick_done, same_done = sem("pick_done"), sem("same_done")
        prod_done, msg_done = sem("prod_done"), sem("msg_done")
        moved_done, idx_done = sem("moved_done"), sem("idx_done")
        sum_out = sem("sum_copied")
        landed = [sem(f"landed{b}") for b in range(NACC)]
        col2_ps, col2_free, col2_read, dst_cast = (sem(n) for n in ("col2_ps", "col2_free", "col2_read", "dst_cast"))
        tg_step = sem("tg_step")
        didx_done = sem("didx_done")
        scatter_turn, gather_turn = sem("scatter_turn"), sem("gather_turn")
        fin_in = [sem(f"fin_in{b}") for b in range(NACC)]
        fin_add, fin_out = sem("fin_add"), sem("fin_out")
        START = [32] + [16] * (NACC - 1)

        half_cols = [slice(H0[a] * P, (H0[a] + HT[a]) * P) for a in range(2)]

        def run_steps(eng, step, lead, lag):
            head = 6
            first = head // 2
            end = ROUNDS - 2 - (ROUNDS - 2 - first) % 2
            for h in range(-lead, head):
                step(h, h % 4, h // 2)
            with eng.Fori(first, end - 1, 2) as i:
                q = eng.snap(i)
                for k in range(4):
                    step(2 * q + k, (2 * first + k) % 4, q + k // 2)
            for h in range(2 * end, LAST + lag + 1):
                step(h, h % 4, h // 2)

        def inside(h, d):
            return not isinstance(h, int) or 0 <= h + d <= LAST

        def wait_half(eng, s, h, per=1):
            if not isinstance(h, int) or h >= 0:
                eng.wait_ge(s, h * per + per)

        def wait_slot(eng, s, h, slot, ring):
            if isinstance(h, int):
                eng.wait_ge(s, 16 * (h // ring + 1))
            else:
                eng.wait_ge(s, h * (16 // ring) + (16 - (slot % ring) * (16 // ring)))

        def tiles_of(q, a):
            return q * RT + H0[a]

        def cut(ap, start, n):
            return ap[:, start:start + n] if isinstance(start, int) else ap[:, bass.ds(start, n)]

        def split_v(engine, link, c, left):
            v = attr_n[:, c * RE:(c + 1) * RE, 1]
            s = c % 2
            link(engine.tensor_copy(parts[:, s, 0, :], v))
            link(engine.tensor_tensor(left[:, :], v, parts[:, s, 0, :], ALU.subtract))
            link(engine.tensor_copy(parts[:, s, 1, :], left[:, :]))
            return engine.tensor_tensor(parts[:, s, 2, :], left[:, :], parts[:, s, 1, :], ALU.subtract)

        def wait_zone(eng):
            eng.wait_ge(hp_out, 16)

        def r_bytes(a):
            start = 3 * H0[a] * P
            return rs_n[:, :, start:start + HT[a] * P]

        def src_bytes(a):
            start = 3 * H0[a] * P + HT[a] * P
            return rs_n[:, :, start:start + 2 * HT[a] * P].bitcast(U16)

        def fin_buf(b):
            if b < 3:
                part = NN * F // KU
                return tent_u[0:NP, b * part:(b + 1) * part, :].rearrange("p t i -> p (t i)")
            part = NN * F // 2
            return attr_n[:, (b - 3) * part:(b - 2) * part, :].rearrange("p e c -> p (e c)")

        block = ctx.enter_context(nc.Block())

        @block.sync
        def _(sp):
            sp.dma_start(x_n, x.rearrange("(p n) f -> p (n f)", p=NP)).then_inc(ld_x, 16)
            sp.dma_start(src_n[:, :], src.rearrange("(p e) -> p e", p=NP)).then_inc(ld_src, 16)
            sp.dma_start(attr_n[:, :, :], attr.rearrange("(p e) c -> p e c", p=NP)).then_inc(ld_attr, 16)
            sp.dma_start(dst_n[:, :], dst.rearrange("(p e) -> p e", p=NP)).then_inc(ld_dst, 16)
            for i in range(KU):
                sp.dma_start(w_sb[:, i, :], weight[i].rearrange("j f o -> (j f) o")).then_inc(ld_w, 16)
            sp.wait_ge(base_done, 1)
            sp.dma_start(base_d.rearrange("o (p r c) -> (o p) r c", p=NP, r=RP), base_i[:, :, :]).then_inc(base_out, 16)
            vrow_v = vrow_d.rearrange("k (p c e) -> p k c e", p=NP, c=RP)
            for c in range(RP):
                if c == PC:
                    sp.wait_ge(hp_done, 1)
                    sp.dma_start(hp_d.rearrange("(p n) c -> p (n c)", p=NP),
                                 h_parts.rearrange("p n k f -> p (n k f)")).then_inc(hp_out, 16)
                if c == RP - 1:
                    sp.wait_ge(rs_cast, 2)
                    sp.dma_start(rs_d.rearrange("(p r) c -> p r c", p=NP), rs_n[:, :, :]).then_inc(rs_out, 16)
                if c < PC:
                    sp.wait_ge(part_done, c + 1)
                else:
                    sp.wait_ge(part_done_v, c - PC + 1)
                sp.dma_start(vrow_v[:, :, c, :], parts[:, c % 2, :, :]).then_inc(part_out[c % 2], 16)

            sp.wait_ge(base_out, 16)
            sp.wait_ge(far_ready, 1)
            sp.dma_start(base_row, base_d).then_inc(base_in, 16)
            sp.wait_ge(rs_out, 16)
            for i in range(2):
                sp.wait_ge(part_out[i], 16 * len(range(i, RP, 2)))
            wait_zone(sp)
            sp.wait_ge(base_in, 16)

            hp_w = hp_d.rearrange("n (k f) -> (n k) f", k=NPART)

            def load_v(h, slot, q):
                start = tiles_of(q, slot % 2) * P
                cols = HT[slot % 2] * P
                wait_half(sp, v_ps, h - 4)
                sp.dma_start(vrow[slot][:, 0:cols], cut(vrow_d, start, cols)).then_inc(s_vrow[slot], 16)

            def load_windows(h, slot, q):
                bases = [sp.value_load(cut(base_row, 2 * q + a, 1), min_val=0, max_val=N - WIN) for a in range(2)]
                blocks = [hp_w[bass.ds(base * NPART, WR), :].unsqueeze(1).to_broadcast([WR, KV, F]) for base in bases]
                for a in range(2):
                    wait_half(sp, h_ps, h + a - 4)
                    sp.dma_start(win[slot + a].rearrange("p (j f) -> p j f", f=F), blocks[a])\
                      .then_inc(s_win[slot + a], 16)

            def step(h, slot, q):
                if inside(h, 3):
                    load_v(h + 3, (slot + 3) % 4, q + 1 + slot % 2)
                if slot % 2 == 0 and inside(h, 2):
                    load_windows(h + 2, (slot + 2) % 4, q + 1)

            far = sp.value_load(far_i[0:1, 0:1], min_val=0, max_val=1)
            with sp.If(far == 0):
                run_steps(sp, step, 3, 0)
            with sp.Else():
                sp.dma_start(h_d.rearrange("(p n) f -> p (n f)", p=NP), x_n).then_inc(h_out, 16)

            for b in range(NACC):
                sp.wait_ge(landed[b], START[b] + 16 * ROUNDS)
                dest = fin_buf(b)
                sp.dma_start(dest, acc_d[b][0:N, :].rearrange("(p n) f -> p (n f)", p=NP)).then_inc(fin_in[b], 16)
            sp.wait_ge(fin_add, NACC - 1)
            sp.dma_start(out.rearrange("(p n) f -> p (n f)", p=NP), fin_buf(0)).then_inc(fin_out, 16)
            sp.wait_ge(fin_out, 16)

        @block.gpsimd
        def _(pool):
            steps = [0]

            def chain(ins):
                ins.then_inc(const_step, 1)
                steps[0] += 1
                pool.wait_ge(const_step, steps[0])

            nc.gpsimd.memset(zero[:, :], 0.0).then_inc(zero_ready, 1)
            chain(nc.gpsimd.memset(ident[:, :], 0.0))
            chain(nc.gpsimd.affine_select(out=ident[:, :], in_=ident[:, :], compare_op=ALU.not_equal, fill=1.0,
                                          base=0, pattern=[[-1, P]], channel_multiplier=1))
            chain(nc.gpsimd.memset(tri[:, :], 1.0))
            chain(nc.gpsimd.affine_select(out=tri[:, :], in_=tri[:, :], compare_op=ALU.is_ge, fill=0.0,
                                          base=0, pattern=[[-1, P]], channel_multiplier=1))
            chain(nc.gpsimd.memset(ones_bf[:, :], 1.0))
            chain(nc.gpsimd.iota(int_col[:, 0:1], pattern=[[0, 1]], base=0, channel_multiplier=1))
            nc.gpsimd.tensor_scalar(dummy_col[:, :], int_col[:, 0:1], float(N), None, ALU.add).then_inc(const_ready, 1)

            rest_rows = AROWS - N
            zp = max(d for d in range(1, P + 1) if rest_rows % d == 0)
            zsrc = zero[:, :].unsqueeze(1).to_broadcast([P, 4, AR * FO // 4])

            def start_accumulator(b):
                if b == 0:
                    pool.dma_start(acc_d[0][0:N, :].rearrange("(p n) f -> p (n f)", p=NP),
                                   x.rearrange("(p n) f -> p (n f)", p=NP)).then_inc(landed[0], 16)
                    pool.dma_start(acc_d[0][N:AROWS, :].rearrange("(p n) f -> p (n f)", p=zp),
                                   zero[0:zp, 0:rest_rows // zp * FO]).then_inc(landed[0], 16)
                else:
                    pool.dma_start(acc_d[b].rearrange("(p k n) f -> p k (n f)", p=P, k=4), zsrc)\
                      .then_inc(landed[b], 16)

            pool.wait_ge(zero_ready, 1)
            pool.wait_ge(ld_attr, 16)
            n = [0]

            def link(ins):
                ins.then_inc(part_step, 1)
                n[0] += 1
                pool.wait_ge(part_step, n[0])

            starts = ((0, 1), (2,), (3, 4))
            assert len(starts) == PC and sum(map(len, starts)) == NACC
            for c in range(PC):
                if c >= 2:
                    pool.wait_ge(part_out[c % 2], 16 * (c // 2))
                split_v(nc.gpsimd, link, c, rest_p).then_inc(part_done, 1)
                pool.wait_ge(part_done, c + 1)
                for b in starts[c]:
                    start_accumulator(b)
            wait_zone(pool)
            pool.wait_ge(far_ready, 1)

            def scatter(h, slot, q):
                a = slot % 2
                wait_half(pool, sum_out, h)
                wait_half(pool, idx_done, h)
                for b in range(H0[a], H0[a] + HT[a]):
                    pool.wait_ge(landed[b], q * 16 + START[b])
                pool.sem_inc(scatter_turn, 1)
                for t in range(HT[a]):
                    b = H0[a] + t
                    k = (slot // 2) * RT + b
                    idx = row_idx[:, k:k + 1]
                    pool.indirect_dma_start(acc_d[b], bass.IndirectOffsetOnAxis(ap=idx, axis=0),
                                            summed[k], None,
                                            compute_op=ALU.add).then_inc(landed[b], 16)

            def gather_scatter(h, slot, q):
                if inside(h, 3):
                    a = (slot + 3) % 2
                    slot3 = (slot + 3) % 4
                    wait_half(pool, pick_done, h + 1)
                    wait_half(pool, didx_done, h + 3)
                    pool.sem_inc(gather_turn, 1)
                    for t in range(HT[a]):
                        k = slot3 * HT[0] + t
                        idx = dst_idx[:, k:k + 1]
                        pool.indirect_dma_start(hg[a][:, t * F:(t + 1) * F], None, h_d,
                                                bass.IndirectOffsetOnAxis(ap=idx, axis=0)).then_inc(s_gat[a], 16)
                if inside(h, -1):
                    scatter(h - 1, (slot - 1) % 4, q - 1 + slot % 2)

            far = pool.value_load(far_i[0:1, 0:1], min_val=0, max_val=1)
            with pool.If(far == 0):
                run_steps(pool, scatter, 0, 0)
            with pool.Else():
                pool.wait_ge(h_out, 16)
                run_steps(pool, gather_scatter, 3, 1)

        NCB = -(-TP // 4)

        def col_bank(c, k):
            return bank[4 + 2 * (c % 2) + k]

        def columns(c):
            m = min(4, TP - 4 * c)
            return m

        @block.scalar
        def _(act):
            act.wait_ge(ld_src, 16)
            nc.scalar.copy(src_f[:, :], src_n[:, :]).then_inc(src_cast, 1)
            act.wait_ge(ln_step, 3)
            nc.scalar.activation(sq_n, x_n, ACT.Square).then_inc(ln_step, 1)
            for a in range(2):
                last = nc.scalar.copy(src_bytes(a), src_n[:, :].rearrange("p (r e) -> p r e", r=RP)[:, :, half_cols[a]])
            last.then_inc(rs_cast, 1)
            act.wait_ge(ln_step, 5)
            nc.scalar.activation(stat[:, 1, :], stat[:, 2, :], ACT.Sqrt, bias=eps_col[0:NP, :], scale=1.0 / F)\
              .then_inc(ln_step, 1)
            act.wait_ge(const_ready, 2)
            for c in range(NCB):
                m = columns(c)
                act.wait_ge(col_ps, 2 * c + 1)
                dest = src_col[:, :].rearrange("p (a k) -> p k a", k=TP)[:, 4 * c:4 * c + m, :]
                nc.scalar.copy(dest, col_bank(c, 0)[:, 0:m * NP].rearrange("p (k a) -> p k a", k=m))\
                  .then_inc(col_read, 1)
                act.wait_ge(col_ps, 2 * c + 2)
                for i in range(KU):
                    dest = tent_u[:, :, i].rearrange("p (a k) -> p k a", k=TP)[:, 4 * c:4 * c + m, :]
                    last = nc.scalar.activation(dest, col_bank(c, 1)[:, 0:m * NP].rearrange("p (k a) -> p k a", k=m),
                                                ACT.Abs, bias=cu[:, i:i + 1], scale=1.0)
                last.then_inc(col_read, 1)
            act.wait_ge(r_done, 1)
            for a in range(2):
                last = nc.scalar.copy(r_bytes(a), r_n[:, :].rearrange("p (r e) -> p r e", r=RP)[:, :, half_cols[a]])
            last.then_inc(rs_cast, 1)
            act.wait_ge(col_read, 2 * NCB)
            flat = tent_u[:, :, :].rearrange("p t i -> p (t i)")
            nc.scalar.activation(flat, flat, ACT.Relu, bias=ones_col[:, :], scale=-SLOPE).then_inc(tent_u_done, 1)
            act.wait_ge(rs_out, 16)
            wait_zone(act)
            act.wait_ge(far_ready, 1)

            rs_line = rs_d.rearrange("(o r) c -> o (r c)", o=1)

            def load_rs(h, slot, q):
                n = 3 * HT[slot % 2] * P
                line = cut(rs_line, q * (3 * RE) + 3 * H0[slot % 2] * P, n).to_broadcast([P, n])
                wait_half(act, same_done, h - 4)
                act.dma_start(rs[slot][:, 0:n], line).then_inc(s_rs[slot], 16)

            def tents(h, slot):
                a = slot % 2
                cols = HT[a] * P
                wait_half(act, v_ps, h)
                wait_half(act, tv_done, h - 2)
                nc.scalar.activation(dist[a][:, 0:cols], ps_v[a], ACT.Abs, bias=cv_col[:, :], scale=1.0)\
                  .then_inc(dist_done, 1)
                wait_half(act, gv_done, h - 4)
                wait_half(act, dist_done, h)
                nc.scalar.activation(tent_v[slot][:, 0:cols], dist[a][:, 0:cols], ACT.Relu,
                                     bias=ones_col[:, :], scale=-SLOPE).then_inc(tv_done, 1)

            def copy_sums(h, slot, q):
                a = slot % 2
                wait_half(act, m_ps, h)
                if not isinstance(h, int) or h >= 4:
                    for b in range(H0[a], H0[a] + HT[a]):
                        act.wait_ge(landed[b], q * 16 + START[b] - 16)
                for t in range(HT[a]):
                    ins = nc.scalar.copy(summed[(slot // 2) * RT + H0[a] + t], ps_m[a][:, t * FO:(t + 1) * FO])
                ins.then_inc(sum_out, 1)

            def step(h, slot, q, windows=True):
                if inside(h, 3):
                    load_rs(h + 3, (slot + 3) % 4, q + 1 + slot % 2)
                if inside(h, -3):
                    copy_sums(h - 3, (slot - 3) % 4, q - 2 + slot % 2)
                if windows and inside(h, 2):
                    tents(h + 2, (slot + 2) % 4)

            far = act.value_load(far_i[0:1, 0:1], min_val=0, max_val=1)
            with act.If(far == 0):
                run_steps(act, step, 3, 3)
            with act.Else():
                act.wait_ge(h_out, 16)
                run_steps(act, lambda h, slot, q: step(h, slot, q, False), 3, 3)

        @block.vector
        def _(dve):
            nc.vector.memset(ones_col[:, :], 1.0)
            nc.vector.memset(eps_col[:, :], EPS)
            for i in range(KU):
                last = nc.vector.memset(cu[:, i:i + 1], 1.0 - 2.0 * i / (KU - 1))
            last.then_inc(const_ready, 1)
            dve.wait_ge(ld_x, 16)
            x3 = x_n.rearrange("p (n f) -> p n f", f=F)
            sq3 = sq_n.rearrange("p (n f) -> p n f", f=F)
            wide = [NP, NN, F]
            nc.vector.tensor_reduce(stat[:, 0, :], x3, AX.X, ALU.add).then_inc(ln_step, 1)
            dve.wait_ge(ln_step, 1)
            nc.vector.tensor_scalar(stat[:, 1, :], stat[:, 0, :], 1.0 / F, None, ALU.mult).then_inc(ln_step, 1)
            dve.wait_ge(ln_step, 2)
            nc.vector.tensor_tensor(x3, x3, stat[:, 1, :].unsqueeze(2).to_broadcast(wide), ALU.subtract)\
              .then_inc(ln_step, 1)
            dve.wait_ge(ln_step, 4)
            nc.vector.tensor_reduce(stat[:, 2, :], sq3, AX.X, ALU.add).then_inc(ln_step, 1)
            dve.wait_ge(ln_step, 6)
            nc.vector.reciprocal(stat[:, 0, :], stat[:, 1, :]).then_inc(ln_step, 1)
            dve.wait_ge(ln_step, 7)
            nc.vector.scalar_tensor_tensor(out=x3, in0=x3, scalar=0.0,
                                           in1=stat[:, 0, :].unsqueeze(2).to_broadcast(wide),
                                           op0=ALU.max, op1=ALU.mult).then_inc(ln_done, 1)
            dve.wait_ge(const_ready, 2)
            nc.vector.tensor_scalar(int_col[:, 1:2], int_col[:, 0:1], 43.0, None, ALU.mult)
            nc.vector.tensor_scalar(int_col[:, 3:4], int_col[:, 0:1], F.bit_length() - 1, None, ALU.arith_shift_right)\
              .then_inc(r_step, 1)
            dve.wait_ge(r_step, 1)
            nc.vector.tensor_scalar(int_col[:, 2:3], int_col[:, 1:2], 7, None, ALU.arith_shift_right)\
              .then_inc(r_step, 1)
            dve.wait_ge(r_step, 2)
            nc.vector.tensor_copy(node_col[:, :], int_col[:, 2:3]).then_inc(r_step, 1)
            dve.wait_ge(r_step, 3)
            nc.vector.tensor_scalar(cv_col[:, :], int_col[:, 3:4], -2.0 / (KV - 1), 1.0, ALU.mult, ALU.add)\
              .then_inc(r_step, 1)
            dve.wait_ge(ld_dst, 16)
            d5 = dst_n[:, :].rearrange("p (r t e) -> p r t e", r=RP, t=RT)
            for a in range(2):
                nc.vector.tensor_scalar(base_f[:, :, a], d5[:, :, H0[a], 0], float(N - WIN), None, ALU.min)
                last = nc.vector.tensor_scalar(base_i[:, :, a], d5[:, :, H0[a], 0], float(N - WIN), None, ALU.min)
            last.then_inc(base_done, 1)
            dve.wait_ge(base_done, 1)
            dr = dst_n[:, :].rearrange("p (r c) -> p r c", r=RP)
            rr = r_n[:, :].rearrange("p (r c) -> p r c", r=RP)
            for a in range(2):
                last = nc.vector.tensor_tensor(rr[:, :, half_cols[a]], dr[:, :, half_cols[a]],
                                               base_f[:, :, a:a + 1].to_broadcast([NP, RP, HT[a] * P]), ALU.subtract)
            last.then_inc(r_done, 1)
            dve.wait_ge(r_done, 1)
            nc.vector.tensor_reduce(span[:, 0:1], r_n[:, :], AX.X, ALU.min)
            nc.vector.tensor_reduce(span[:, 1:2], r_n[:, :], AX.X, ALU.max).then_inc(r_step, 1)
            dve.wait_ge(r_step, 5)
            nc.vector.tensor_scalar(span[:, 0:1], span[:, 0:1], 0.0, None, ALU.is_lt)
            nc.vector.tensor_scalar(span[:, 1:2], span[:, 1:2], float(WIN - 1), None, ALU.is_gt).then_inc(r_step, 1)
            dve.wait_ge(r_step, 6)
            nc.vector.tensor_tensor(span[:, 2:3], span[:, 0:1], span[:, 1:2], ALU.add).then_inc(r_step, 1)
            dve.wait_ge(ln_done, 1)
            left = sq_n.rearrange("p (n f) -> p n f", f=F)
            nc.vector.tensor_copy(h_parts[:, :, 0, :], x3).then_inc(hp_step, 1)
            dve.wait_ge(hp_step, 1)
            nc.vector.tensor_tensor(left, x3, h_parts[:, :, 0, :], ALU.subtract).then_inc(hp_step, 1)
            dve.wait_ge(hp_step, 2)
            nc.vector.tensor_copy(h_parts[:, :, 1, :], left).then_inc(hp_step, 1)
            dve.wait_ge(hp_step, 3)
            nc.vector.tensor_tensor(h_parts[:, :, 2, :], left, h_parts[:, :, 1, :], ALU.subtract).then_inc(hp_done, 1)
            dve.wait_ge(ld_attr, 16)
            links = [0]

            def link(ins):
                ins.then_inc(part_step_v, 1)
                links[0] += 1
                dve.wait_ge(part_step_v, links[0])

            for c in range(PC, RP):
                dve.wait_ge(part_out[c % 2], 16 * (c // 2))
                split_v(nc.vector, link, c, rest_v).then_inc(part_done_v, 1)
                dve.wait_ge(part_done_v, c - PC + 1)
            dve.wait_ge(far_ps, 1)
            nc.vector.tensor_scalar(far_i[0:1, 0:1], bank[0][0:1, 0:1], 1.0, None, ALU.min).then_inc(far_ready, 1)
            dve.wait_ge(far_ready, 1)
            wait_zone(dve)
            dve.wait_ge(tent_u_done, 1)

            def build_pick(h, slot, q):
                cols = HT[slot % 2] * P
                wait_slot(dve, s_rs[slot], h, slot, 4)
                wait_half(dve, h_ps, h - 4)
                nc.vector.tensor_scalar(pick[slot][:, 0:cols], r_row(slot), node_col[0:WR, :], None, ALU.is_equal)\
                  .then_inc(pick_done, 1)

            def weigh_v(h, slot):
                a = slot % 2
                cols = HT[a] * P
                wait_half(dve, h_ps, h)
                wait_half(dve, g_ps, h - 4)
                if far_form[0]:
                    nc.vector.tensor_copy(gv[slot][:, 0:cols], ps_h[a]).then_inc(gv_done, 1)
                else:
                    wait_half(dve, tv_done, h)
                    nc.vector.tensor_tensor(gv[slot][:, 0:cols], ps_h[a], tent_v[slot][:, 0:cols], ALU.mult)\
                      .then_inc(gv_done, 1)

            def build_same(h, slot, q):
                a = slot % 2
                wait_slot(dve, s_rs[slot], h, slot, 4)
                wait_half(dve, m_ps, h - 4)
                wait_half(dve, moved_done, h - 4)
                for t in range(HT[a]):
                    ins = nc.vector.scalar_tensor_tensor(
                        out=same[slot][:, t * P:(t + 1) * P], in0=src_row(slot, t),
                        scalar=cut(src_col, tiles_of(q, a) + t, 1), in1=tri[:, :],
                        op0=ALU.is_equal, op1=ALU.mult, accum_out=count[slot][:, t:t + 1])
                ins.then_inc(same_done, 1)

            def weigh(h, slot, q):
                a = slot % 2
                n = HT[a]
                g_in = ps_g[a]
                wait_half(dve, g_ps, h)
                wait_half(dve, msg_done, h - 2)
                tu = cut(tent_u, tiles_of(q, a), n).rearrange("p t i -> p (t i)")
                nc.vector.tensor_tensor(prod[a][:, 0:n * IO].rearrange("p (k o) -> p k o", o=FO),
                                        g_in.rearrange("p (k o) -> p k o", o=FO),
                                        tu.unsqueeze(2).to_broadcast([P, n * KU, FO]), ALU.mult).then_inc(prod_done, 1)

            def sum_i(h, slot):
                a = slot % 2
                n = HT[a]
                wait_half(dve, prod_done, h)
                wait_half(dve, m_ps, h - 4)
                nc.vector.tensor_reduce(msg[slot][:, 0:n * FO].rearrange("p (t o) -> p t o", o=FO),
                                        prod[a][:, 0:n * IO].rearrange("p (t i o) -> p t o i", t=n, i=KU),
                                        AX.X, ALU.add).then_inc(msg_done, 1)

            def mark_repeats(h, slot):
                a = slot % 2
                n = HT[a]
                wait_half(dve, same_done, h)
                wait_half(dve, idx_done, h - 4)
                nc.vector.scalar_tensor_tensor(out=moved[slot][:, 0:n], in0=count[slot][:, 0:n], scalar=1.0,
                                               in1=dummy_col[:, :].to_broadcast([P, n]),
                                               op0=ALU.is_gt, op1=ALU.mult).then_inc(moved_done, 1)

            def choose_rows(h, slot, q):
                a = slot % 2
                n = HT[a]
                wait_half(dve, moved_done, h)
                t0 = tiles_of(q, a)
                if not isinstance(h, int) or h >= 4:
                    for b in range(H0[a], H0[a] + n):
                        dve.wait_ge(landed[b], q * 16 + START[b] - 16)
                k = (slot // 2) * RT + H0[a]
                nc.vector.tensor_tensor(row_idx[:, k:k + n], moved[slot][:, 0:n], cut(src_col, t0, n), ALU.max)\
                  .then_inc(idx_done, 1)

            far_form = [False]

            def combine(h, slot, q):
                a = slot % 2
                n = HT[a]
                tg = tent_g[a][:, 0:n * KV].rearrange("p (t j) -> p t j", j=KV)
                wait_half(dve, pick_done, h - 2)
                nc.vector.tensor_tensor(tg, cut(v_col, tiles_of(q, a), n).unsqueeze(2).to_broadcast([P, n, KV]),
                                        cu[:, :].unsqueeze(1).to_broadcast([P, n, KV]), ALU.add).then_inc(tg_step, 1)
                dve.wait_ge(tg_step, h * 4 + 1)
                flat = tent_g[a][:, 0:n * KV]
                nc.vector.tensor_scalar(minus_g[a][:, 0:n * KV], flat, -1.0, None, ALU.mult).then_inc(tg_step, 1)
                dve.wait_ge(tg_step, h * 4 + 2)
                nc.vector.tensor_tensor(flat, flat, minus_g[a][:, 0:n * KV], ALU.max).then_inc(tg_step, 1)
                dve.wait_ge(tg_step, h * 4 + 3)
                nc.vector.tensor_scalar(flat, flat, -SLOPE, 1.0, ALU.mult, ALU.add).then_inc(tg_step, 1)
                dve.wait_ge(tg_step, h * 4 + 4)
                dve.wait_ge(s_gat[a], q * (16 * n) + 16 * n)
                wait_half(dve, h_ps, h - 2)
                for t in range(n):
                    ins = nc.vector.scalar_tensor_tensor(
                        out=hv[a][:, t * P:(t + 1) * P].rearrange("p (j f) -> p j f", f=F),
                        in0=flat[:, t * KV:(t + 1) * KV].unsqueeze(2).to_broadcast([P, KV, F]), scalar=0.0,
                        in1=hg[a][:, t * F:(t + 1) * F].unsqueeze(1).to_broadcast([P, KV, F]),
                        op0=ALU.max, op1=ALU.mult)
                ins.then_inc(pick_done, 1)

            def index_dst(h, slot, q):
                a = slot % 2
                wait_half(dve, pick_done, h - 4)
                nc.vector.tensor_copy(dst_idx[:, slot * HT[0]:slot * HT[0] + HT[a]],
                                      cut(dst_col, tiles_of(q, a), HT[a])).then_inc(didx_done, 1)

            def step(h, slot, q):
                if inside(h, -3):
                    mark_repeats(h - 3, (slot - 3) % 4)
                if inside(h, -2):
                    weigh(h - 2, (slot - 2) % 4, q - 1)
                if inside(h, -3):
                    choose_rows(h - 3, (slot - 3) % 4, q - 2 + slot % 2)
                if inside(h, 0):
                    weigh_v(h, slot)
                if inside(h, -2):
                    sum_i(h - 2, (slot - 2) % 4)
                if inside(h, 2):
                    (combine if far_form[0] else build_pick)(h + 2, (slot + 2) % 4, q + 1)
                if far_form[0] and inside(h, 4):
                    index_dst(h + 4, slot, q + 2)
                if inside(h, 0):
                    build_same(h, slot, q)

            far = dve.value_load(far_i[0:1, 0:1], min_val=0, max_val=1)
            with dve.If(far == 0):
                run_steps(dve, step, 2, 3)
            with dve.Else():
                far_form[0] = True
                dve.wait_ge(h_out, 16)
                for i in range(2):
                    dve.wait_ge(part_out[i], 16 * len(range(i, RP, 2)))
                nc.vector.tensor_copy(dst_f, dst_n[:, :]).then_inc(dst_cast, 1)
                for c in range(NCB):
                    m = columns(c)
                    dve.wait_ge(col2_ps, c + 1)
                    for k, dest in enumerate((dst_col, v_col)):
                        last = nc.vector.tensor_copy(
                            dest.rearrange("p (a k) -> p k a", k=TP)[:, 4 * c:4 * c + m, :],
                            bank[6 + k][:, 0:m * NP].rearrange("p (k a) -> p k a", k=m))
                    if c < NCB - 1:
                        last.then_inc(col2_free, 1)
                    else:
                        last.then_inc(col2_read, 1)
                dve.wait_ge(col2_read, 1)
                run_steps(dve, step, 4, 3)

            dve.wait_ge(fin_in[0], 16)
            for b in range(1, NACC):
                dve.wait_ge(fin_in[b], 16)
                if b >= 2:
                    dve.wait_ge(fin_add, b - 1)
                nc.vector.tensor_tensor(fin_buf(0), fin_buf(0), fin_buf(b), ALU.add).then_inc(fin_add, 1)

        @block.tensor
        def _(pe):
            idn = ident[0:NP, 0:NP]
            pe.wait_ge(const_ready, 2)
            pe.wait_ge(src_cast, 1)
            pe.wait_ge(ld_attr, 16)
            for c in range(NCB):
                m = columns(c)
                for k in range(2):
                    if c >= 2:
                        pe.wait_ge(col_read, 2 * c - 3 + k)
                    for t in range(m):
                        e = slice((4 * c + t) * P, (4 * c + t + 1) * P)
                        ins = nc.tensor.transpose(col_bank(c, k)[:, t * NP:(t + 1) * NP],
                                                  src_f[:, e] if k == 0 else attr_n[:, e, 0], idn)
                    ins.then_inc(col_ps, 1)
            pe.wait_ge(r_step, 7)
            nc.tensor.matmul(bank[0][0:1, 0:1], span[:, 2:3], ones_col[0:NP, :], start=True, stop=True)\
              .then_inc(far_ps, 1)
            pe.wait_ge(far_ready, 1)
            pe.wait_ge(ld_w, 16 * KU)
            pe.wait_ge(col_read, 2 * NCB)

            def broadcast_v(h, slot):
                a = slot % 2
                wait_slot(pe, s_vrow[slot], h, slot, 4)
                wait_half(pe, dist_done, h - 2)
                nc.tensor.matmul(ps_v[a], ones_bf[:, :], vrow[slot][:, 0:HT[a] * P], start=True, stop=True)\
                  .then_inc(v_ps, 1)

            def spread(h, slot):
                a = slot % 2
                wait_half(pe, pick_done, h)
                wait_half(pe, gv_done, h - 2)
                if far_form[0]:
                    for t in range(HT[a]):
                        ins = nc.tensor.transpose(ps_h[a][:, t * P:(t + 1) * P], hv[a][:, t * P:(t + 1) * P],
                                                  ident[:, :])
                    ins.then_inc(h_ps, 1)
                else:
                    wait_slot(pe, s_win[slot], h, slot, 4)
                    nc.tensor.matmul(ps_h[a], win[slot],
                                     pick[slot][:, 0:HT[a] * P], start=True, stop=True).then_inc(h_ps, 1)

            def times_w(h, slot):
                a = slot % 2
                wait_half(pe, gv_done, h)
                wait_half(pe, prod_done, h - 2)
                for t in range(HT[a]):
                    ins = nc.tensor.matmul(ps_g[a][:, t * P:(t + 1) * P], gv[slot][:, t * P:(t + 1) * P],
                                           w_sb[:, :, :].rearrange("p i o -> p (i o)"), start=True, stop=True)
                ins.then_inc(g_ps, 1)

            def sum_same(h, slot):
                a = slot % 2
                wait_half(pe, same_done, h)
                wait_half(pe, msg_done, h)
                wait_half(pe, sum_out, h - 2)
                for t in range(HT[a]):
                    ins = nc.tensor.matmul(ps_m[a][:, t * FO:(t + 1) * FO], same[slot][:, t * P:(t + 1) * P],
                                           msg[slot][:, t * FO:(t + 1) * FO], start=True, stop=True)
                ins.then_inc(m_ps, 1)

            far_form = [False]

            def step(h, slot, q):
                if not far_form[0] and inside(h, 2):
                    broadcast_v(h + 2, (slot + 2) % 4)
                if inside(h, 1):
                    spread(h + 1, (slot + 1) % 4)
                if inside(h, 0):
                    times_w(h, slot)
                if inside(h, -2):
                    sum_same(h - 2, (slot - 2) % 4)

            far = pe.value_load(far_i[0:1, 0:1], min_val=0, max_val=1)
            with pe.If(far == 0):
                run_steps(pe, step, 2, 2)
            with pe.Else():
                far_form[0] = True
                pe.wait_ge(dst_cast, 1)
                for c in range(NCB):
                    m = columns(c)
                    if c >= 1:
                        pe.wait_ge(col2_free, c)
                    for k in range(2):
                        for t in range(m):
                            e = slice((4 * c + t) * P, (4 * c + t + 1) * P)
                            ins = nc.tensor.transpose(bank[6 + k][:, t * NP:(t + 1) * NP],
                                                      dst_f[:, e] if k == 0 else attr_n[:, e, 1], idn)
                    ins.then_inc(col2_ps, 1)
                pe.wait_ge(col2_read, 1)
                run_steps(pe, step, 1, 2)


_INS = ["x", "src", "dst", "edge_attr_2", "L0_gnn_weight"]


def kernel(**inputs):
    import concourse.bacc as _bacc
    from concourse.bass_utils import run_bass_kernel_spmd as _run

    nc = _bacc.Bacc("TRN2", target_bir_lowering=False, num_devices=1)
    arrays, args = {}, []
    for name in _INS:
        a = np.ascontiguousarray(inputs[name])
        arrays[f"in_{name}"] = a
        args.append(nc.dram_tensor(f"in_{name}", a.shape, mybir.dt.from_np(a.dtype), kind="ExternalInput").ap())
    shape = inputs["x"].shape
    args.append(nc.dram_tensor("out_x", shape, F32, kind="ExternalOutput").ap())
    edge_conv_kernel(nc, *args)
    r = _run(nc, [arrays], core_ids=[0])
    return r.results[0]["out_x"]
```
